# Optimizing a Trainium2 kernel written in Bass

```python
import numpy as np
import jax
import jax.numpy as jnp

def _softmax(x, axis=-1):
    return jax.nn.softmax(x, axis=axis)

def _gelu(x):
    return jax.nn.gelu(x, approximate=True)

def _silu(x):
    return jax.nn.silu(x)

def _sigmoid(x):
    return jax.nn.sigmoid(x)

def _layernorm(x, axis=-1, eps=1e-05):
    m = jnp.mean(x, axis=axis, keepdims=True)
    v = jnp.var(x, axis=axis, keepdims=True)
    return (x - m) / jnp.sqrt(v + eps)

def _scatter_add(tgt, idx, src, axis=0):
    return tgt.at[idx].add(src)

def _segment_sum(src, seg, n):
    return jax.ops.segment_sum(src, seg, n)
kernel_name = 'mk_sandwich_d1_jaxref_r4_48c33c'

def setup_inputs(seed: int=0):
    np.random.seed(seed)
    _w = jnp.asarray

    def _L0_attn_setup():
        import jax, jax.numpy as jnp
        import numpy as np
        B, N, D = (8, 256, 1024)
        H = 8
        HEAD_DIM = D // H
        E = HEAD_DIM // H
        key = jax.random.key(seed)
        ks = jax.random.split(key, 7)
        s = 0.02
        return {'x': jax.random.normal(ks[0], (B, N, D), dtype=jnp.float32), 'Wqk_w': jax.random.normal(ks[1], (2 * HEAD_DIM, D), dtype=jnp.float32) * s, 'Wqk_b': jnp.zeros((2 * HEAD_DIM,), dtype=jnp.float32), 'Wv_w': jax.random.normal(ks[2], (HEAD_DIM, D), dtype=jnp.float32) * s, 'Wv_b': jnp.zeros((HEAD_DIM,), dtype=jnp.float32), 'Wo_w': jax.random.normal(ks[3], (D, HEAD_DIM), dtype=jnp.float32) * s, 'Wo_b': jnp.zeros((D,), dtype=jnp.float32)}
    _L0_attn_in = _L0_attn_setup()

    def _L0_ffn_setup():
        import jax, jax.numpy as jnp
        import numpy as np
        B, S, D = (4, 512, 1024)
        NUM_EXPERTS, TOP_K = (3, 2)

        def _expert_outputs(h, w1, b1, w2, b2):
            pre = jnp.einsum('bsd,edf->ebsf', h, w1) + b1[:, None, None, :]
            act = jnp.stack([jnp.tanh(pre[0]), jax.nn.gelu(pre[1], approximate=False), jax.nn.silu(pre[2])])
            return jnp.einsum('ebsf,efd->ebsd', act, w2) + b2[:, None, None, :]
        key = jax.random.key(seed)
        ks = jax.random.split(key, 8)
        scale_in = 1.0 / np.sqrt(D)
        scale_gate = 1.0 / np.sqrt(D + 1)
        return {'h': jax.random.normal(ks[0], (B, S, D), dtype=jnp.float32), 'gate_w': jax.random.uniform(ks[1], (D + 1, NUM_EXPERTS), minval=-scale_gate, maxval=scale_gate, dtype=jnp.float32), 'gate_b': jnp.zeros((NUM_EXPERTS,), dtype=jnp.float32), 'w1': jax.random.uniform(ks[2], (NUM_EXPERTS, D, D), minval=-scale_in, maxval=scale_in, dtype=jnp.float32), 'b1': jnp.zeros((NUM_EXPERTS, D), dtype=jnp.float32), 'w2': jax.random.uniform(ks[3], (NUM_EXPERTS, D, D), minval=-scale_in, maxval=scale_in, dtype=jnp.float32), 'b2': jnp.zeros((NUM_EXPERTS, D), dtype=jnp.float32)}
    _L0_ffn_in = _L0_ffn_setup()
    _d = {'L0_attn_x': _L0_attn_in['x'], 'L0_attn_Wqk_w': _L0_attn_in['Wqk_w'], 'L0_attn_Wqk_b': _L0_attn_in['Wqk_b'], 'L0_attn_Wv_w': _L0_attn_in['Wv_w'], 'L0_attn_Wv_b': _L0_attn_in['Wv_b'], 'L0_attn_Wo_w': _L0_attn_in['Wo_w'], 'L0_attn_Wo_b': _L0_attn_in['Wo_b'], 'L0_ffn_gate_w': _L0_ffn_in['gate_w'], 'L0_ffn_gate_b': _L0_ffn_in['gate_b'], 'L0_ffn_w1': _L0_ffn_in['w1'], 'L0_ffn_b1': _L0_ffn_in['b1'], 'L0_ffn_w2': _L0_ffn_in['w2'], 'L0_ffn_b2': _L0_ffn_in['b2']}
    _x0 = _d['L0_attn_x']
    _d['L0_attn_x'] = jax.random.normal(jax.random.fold_in(jax.random.key(seed), 1), (4, 1024, 1024), dtype=_x0.dtype)
    del _x0
    return _d

def reference(L0_attn_x, L0_attn_Wqk_w, L0_attn_Wqk_b, L0_attn_Wv_w, L0_attn_Wv_b, L0_attn_Wo_w, L0_attn_Wo_b, L0_ffn_gate_w, L0_ffn_gate_b, L0_ffn_w1, L0_ffn_b1, L0_ffn_w2, L0_ffn_b2):

    def _L0_attn_ref(x, Wqk_w, Wqk_b, Wv_w, Wv_b, Wo_w, Wo_b):
        import jax, jax.numpy as jnp
        import numpy as np
        B, N, D = (8, 256, 1024)
        H = 8
        HEAD_DIM = D // H
        E = HEAD_DIM // H
        b, n, _ = x.shape
        qk = (x @ Wqk_w.T + Wqk_b).reshape(b, n, H, E, 2)
        q = jnp.transpose(qk[..., 0], (0, 2, 1, 3))
        k = jnp.transpose(qk[..., 1], (0, 2, 1, 3))
        v = (x @ Wv_w.T + Wv_b).reshape(b, n, H, E)
        v = jnp.transpose(v, (0, 2, 1, 3))
        scores = jnp.einsum('bhqd,bhkd->bhqk', q, k)
        attn = jax.nn.softmax(scores, axis=-1) / jnp.asarray(HEAD_DIM ** 0.5, x.dtype)
        out = jnp.einsum('bhsl,bhlv->bhsv', attn, v)
        out = jnp.transpose(out, (0, 2, 1, 3)).reshape(b, n, H * E)
        return out @ Wo_w.T + Wo_b

    def _L0_ffn_ref(h, gate_w, gate_b, w1, b1, w2, b2):
        import jax, jax.numpy as jnp
        import numpy as np
        B, S, D = (4, 512, 1024)
        NUM_EXPERTS, TOP_K = (3, 2)

        def _expert_outputs(h, w1, b1, w2, b2):
            pre = jnp.einsum('bsd,edf->ebsf', h, w1) + b1[:, None, None, :]
            act = jnp.stack([jnp.tanh(pre[0]), jax.nn.gelu(pre[1], approximate=False), jax.nn.silu(pre[2])])
            return jnp.einsum('ebsf,efd->ebsd', act, w2) + b2[:, None, None, :]
        b, s, d = h.shape
        vision_len = int(s * 0.3)
        text_strength = jnp.mean(jnp.abs(h[:, vision_len:, :]), axis=(1, 2), keepdims=True)
        vision_strength = jnp.mean(jnp.abs(h[:, :vision_len, :]), axis=(1, 2), keepdims=True)
        modality_ratio = text_strength / (vision_strength + 1e-08)
        modality_ratio = jnp.broadcast_to(modality_ratio, (b, s, 1))
        router_input = jnp.concatenate([h, modality_ratio], axis=-1)
        gate_logits = router_input @ gate_w + gate_b
        gate_scores = jax.nn.softmax(gate_logits, axis=-1)
        top_val, top_idx = jax.lax.top_k(gate_scores, TOP_K)
        top_val = top_val / (jnp.sum(top_val, axis=-1, keepdims=True) + 1e-08)
        expert_out = _expert_outputs(h, w1, b1, w2, b2)
        moe_out = jnp.zeros_like(h)
        batch_idx = jnp.arange(b)
        for i in range(TOP_K):
            j = top_idx[:, 0, i]
            out_i = expert_out[j, batch_idx]
            moe_out = moe_out + top_val[..., i:i + 1] * out_i
        return moe_out
    x = L0_attn_x
    x = x + _layernorm(_L0_attn_ref(_layernorm(x, axis=-1), L0_attn_Wqk_w, L0_attn_Wqk_b, L0_attn_Wv_w, L0_attn_Wv_b, L0_attn_Wo_w, L0_attn_Wo_b), axis=-1)
    x = x + _layernorm(_L0_ffn_ref(_layernorm(x, axis=-1), L0_ffn_gate_w, L0_ffn_gate_b, L0_ffn_w1, L0_ffn_b1, L0_ffn_w2, L0_ffn_b2), axis=-1)
    return x

_drawn_inputs = setup_inputs


def setup_inputs(seed=0):
    import zlib

    import numpy as np

    out = dict(_drawn_inputs(seed))
    spreads = {'L0_attn_Wqk_b': (0.0, 0.57),
     'L0_attn_Wv_b': (0.0, 0.519),
     'L0_attn_Wo_b': (0.0, 0.1),
     'L0_ffn_gate_b': (0.0, 0.1),
     'L0_ffn_b1': (0.0, 0.1),
     'L0_ffn_b2': (0.0, 0.1)}
    factors = {}
    for name, (base, spread) in spreads.items():
        noise = np.random.default_rng([zlib.crc32(name.encode()), seed]).standard_normal(out[name].shape)
        drawn = base * np.exp(spread * noise) if base else spread * noise
        out[name] = jnp.asarray(drawn.astype(out[name].dtype))
    for name, factor in factors.items():
        out[name] = (out[name] * factor).astype(out[name].dtype)
    return out
```

```python
from contextlib import ExitStack

import concourse.bass as bass
from concourse import mybir

ALU = mybir.AluOpType
ACT = mybir.ActivationFunctionType
AX = mybir.AxisListType
F32 = mybir.dt.float32
F16 = mybir.dt.float16
I32 = mybir.dt.int32

P = 128
NB, NT, D = 4, 1024, 1024
TT = NT // P
DC = D // P
H, E = 8, 16
HD = H * E
HP = H // 2
HR = P // 2
NE = 3
BANK = 512
HALF = NT // BANK
GRP = 4
NG = TT // GRP
VISION = int(NT * 0.3)
SPLIT_TILE, SPLIT_ROW = VISION // P, VISION % P
EPS = 1e-5
WS = 64.0
STAGE = 4


def add_credits(eng, pairs):
    for sem, n in pairs:
        eng.sem_inc(sem, n)


def wait_apart(eng, sem, value, passed):
    eng.wait_ge(sem, value)
    eng.sem_inc(passed, 1)


def again(eng, value, stage):
    with eng.register(f"batch_{stage}") as reg:
        eng.reg_mov(reg, value)
        return eng.snap(reg, min_val=0, max_val=NB - 1)


def attention_phase(nc, io, scr, keep, ctx):

    def sb(name, shape, dt=F32):
        return ctx.enter_context(nc.sbuf_tensor(name, shape, dt))

    def sem(name):
        return ctx.enter_context(nc.semaphore(name))

    ps = ctx.enter_context(nc.psum_tensor("ps", [P, 8, BANK], F32))

    ident = sb("ident", [P, P])
    ones = sb("ones", [P, P])
    vision_rows = sb("vision_rows", [P, 1])
    half_neg = sb("half_neg", [P, GRP])
    wstage = sb("wstage", [P, 3 * HD])
    gstage = sb("gstage", [P, DC, NE])
    wqkv = [sb(f"wqkv{i}", [P, DC, 3 * HD], F16) for i in range(2)]
    wo = [sb(f"wo{i}", [P, D], F16) for i in range(2)]
    gw = [sb(f"gw{i}", [P, DC, NE], F16) for i in range(2)]
    bqk = sb("bqk", [P, 2])
    bv = sb("bv", [P, HD])
    bo = sb("bo", [P, D])
    gw_ratio = sb("gw_ratio", [P, NE])
    gate_b = sb("gate_b", [P, NE])
    xin = sb("xin", [P, TT, D])
    xn = sb("xn", [P, 2, D])
    xt = [sb(f"xt{i}", [P, DC, NT], F16) for i in range(2)]
    qk32 = sb("qk32", [P, 2, BANK])
    qks = [[sb(f"qks{m}{i}", [P, NT], F16) for i in range(2)] for m in range(2)]
    qa = sb("qa", [P, HP, NT], F16)
    kz = sb("kz", [P, H, NT], F16)
    v32 = sb("v32", [P, TT, H, 32])
    mrow = sb("mrow", [P, P])
    zeros = sb("zeros", [2, HP, NT], F16)
    ms = [sb(f"ms{i}", [P, P], F16) for i in range(2)]
    p32 = sb("p32", [P, 4, 2, BANK])
    osb = sb("osb", [P, 2, BANK])
    rinv = sb("rinv", [P, 4, 4, 1])
    onorm = sb("onorm", [P, TT, HD])
    ot = [sb(f"ot{i}", [P, 2, P], F16) for i in range(2)]
    y4 = sb("y4", [P, GRP, D])
    stats = sb("stats", [P, GRP, 2, 6])
    mv = sb("mv", [P, GRP, 2])
    vare = sb("vare", [P, GRP])
    rstd = sb("rstd", [P, GRP])
    habs = sb("habs", [P, D])
    asum = sb("asum", [P, TT])
    parts = sb("parts", [P, 2])
    gs = sb("gs", [P, 8])
    gbase = sb("gbase", [P, NE])
    lg = sb("lg", [P, TT, NE])
    sc = sb("sc", [P, TT, NE])
    g1 = sb("g1", [P, 8, TT])
    jt = sb("jt", [1, 16])

    const_in = sem("const_in")
    wchunk_in = sem("wchunk_in")
    wchunk_split = sem("wchunk_split")
    pool_consts = sem("pool_consts")
    x_landed = [sem(f"x_landed{g}") for g in range(NG)]
    dve_step = sem("dve_step")
    stat_ready = sem("stat_ready")
    pool_step = sem("pool_step")
    rstd_ready = sem("rstd_ready")
    xn_ready = sem("xn_ready")
    tp_done = sem("tp_done")
    hi_done = sem("hi_done")
    lo_done = sem("lo_done")
    v_mm = sem("v_mm")
    v_done = sem("v_done")
    qk_mm = sem("qk_mm")
    qk32_ready = sem("qk32_ready")
    qk_split = sem("qk_split")
    qk_stored = sem("qk_stored")
    qk_placed = sem("qk_placed")
    s_mm = sem("s_mm")
    s_free = sem("s_free")
    mt_done = sem("mt_done")
    mhi_done = sem("mhi_done")
    mlo_done = sem("mlo_done")
    m_stored = sem("m_stored")
    m_placed = sem("m_placed")
    st_ready = sem("st_ready")
    exp_done = sem("exp_done")
    pv_done = sem("pv_done")
    o_copied = sem("o_copied")
    ot_done = sem("ot_done")
    o_norm = sem("o_norm")
    oo_done = sem("oo_done")
    oohi_done = sem("oohi_done")
    oolo_done = sem("oolo_done")
    y_mm = sem("y_mm")
    y_done = sem("y_done")
    x1_done = sem("x1_done")
    x1_stored = sem("x1_stored")
    ht_stored = sem("ht_stored")
    abs_done = sem("abs_done")
    gate_mm = sem("gate_mm")
    sums_ready = sem("sums_ready")
    sums_mm = sem("sums_mm")
    lg_ready = sem("lg_ready")
    lg_exp = sem("lg_exp")
    gate_done = sem("gate_done")
    passed = sem("passed")

    x_v = io["x"].rearrange("b (t p) d -> b p t d", p=P)
    x1_v = scr["x1"].rearrange("b (t p) d -> b p t d", p=P)
    wqkv_v = io["wqkv_t"].rearrange("(c p) n -> c p n", p=P)
    NCONST = 8
    POOL_CONSTS = 8 + H
    PLACES = 14
    STATS = 6

    def one(ap, b):
        return ap[bass.ds(b, 1)].rearrange("o p t d -> (o p) t d")

    block = ctx.enter_context(nc.Block())

    @block.sync
    def _(sp):
        sp.dma_start(bqk[:], io["bqk"]).then_inc(const_in, 16)
        sp.dma_start(bv[:], io["bv"].partition_broadcast(P)).then_inc(const_in, 16)
        sp.dma_start(bo[:], io["bo"].partition_broadcast(P)).then_inc(const_in, 16)
        sp.dma_start(gw_ratio[:], io["gw_ratio"].partition_broadcast(P)).then_inc(const_in, 16)
        sp.dma_start(gate_b[:], io["gate_b"].partition_broadcast(P)).then_inc(const_in, 16)
        sp.dma_start(gstage[:], io["gate_w"].rearrange("(c p) e -> p c e", p=P)).then_inc(const_in, 16)
        sp.dma_start(y4[:, 0, :], io["wo_t"]).then_inc(const_in, 16)
        sp.dma_start(keep["b1"][:], io["b1"]).then_inc(const_in, 16)
        for c in range(DC):
            if c:
                sp.wait_ge(wchunk_split, c + 2)
            sp.dma_start(wstage[:], wqkv_v[c]).then_inc(wchunk_in, 16)
        with sp.Fori(0, NB) as b:
            sp.wait_ge(x1_done, b * TT + 1)
            for g in range(NG):
                sp.dma_start(xin[:, g * GRP:(g + 1) * GRP, :], one(x_v, b)[:, g * GRP:(g + 1) * GRP, :]
                             ).then_inc(x_landed[g], 16)
            sp.wait_ge(qk_placed, b * (PLACES * 16) + 1)
            sp.wait_ge(qk_split, (b + 1) * 4 + 2)
            for m in range(2):
                for i in range(2):
                    sp.dma_start(scr["qk"][m, i], qks[m][i][:]).then_inc(qk_stored, 16)
            sp.wait_ge(qk_stored, (b + 1) * 64 + 1)
            sp.wait_ge(pv_done, b * 64 + 4)
            for j in range(2):
                for slot in range(3):
                    r = j * HR + slot * E
                    qpart, kpart = slot % 2, slot // 2
                    src = scr["qk"].rearrange("m i (hp j e) t -> m i j e hp t", hp=HP, j=2)
                    sp.dma_start(qa[r:r + E], src[0, qpart, j]).then_inc(qk_placed, 16)
                    kdst = kz[r:r + E].rearrange("e (hp j) t -> e j hp t", j=2)[:, j]
                    sp.dma_start(kdst, src[1, kpart, j]).then_inc(qk_placed, 16)
                r = j * HR + 3 * E
                sp.dma_start(qa[r:r + 2], zeros[0:2]).then_inc(qk_placed, 16)
            sp.wait_ge(mlo_done, b + 1)
            for i in range(2):
                sp.dma_start(scr["m"][i], ms[i][0:H * TT, :]).then_inc(m_stored, 16)
            sp.wait_ge(m_stored, (b + 1) * 32 + 1)
            for i in range(2):
                for j in range(2):
                    r = j * HR + 3 * E + i
                    src = scr["m"].rearrange("i (hp j q) n -> i j hp (q n)", hp=HP, j=2)[i, j]
                    sp.dma_start(qa[r:r + 1], src.unsqueeze(0)).then_inc(m_placed, 16)
            for g in range(NG):
                sp.wait_ge(x1_done, b * TT + (g + 1) * GRP + 1)
                sp.dma_start(one(x1_v, b)[:, g * GRP:(g + 1) * GRP, :], y4[:]).then_inc(x1_stored, 16)
            wait_apart(sp, lo_done, (b + 1) * (2 * TT) + 2, passed)
            for i in range(2):
                sp.dma_start(one(scr["ht"][i], b), xt[i][:]).then_inc(ht_stored, 16)
        sp.wait_ge(ht_stored, NB * 32 + 1)
        sp.wait_ge(x1_stored, NB * NG * 16 + 1)

    @block.gpsimd
    def _(pool):
        nc.gpsimd.memset(ident[:], 0.0).then_inc(pool_step, 1)
        pool.wait_ge(pool_step, 1)
        nc.gpsimd.affine_select(out=ident[:], in_=ident[:], compare_op=ALU.not_equal, fill=1.0, base=0,
                                pattern=[[-1, P]], channel_multiplier=1).then_inc(pool_consts, 1)
        nc.gpsimd.memset(ones[:], 1.0).then_inc(pool_consts, 1)
        nc.gpsimd.memset(half_neg[:], -0.5).then_inc(pool_consts, 1)
        nc.gpsimd.memset(vision_rows[:], 1.0).then_inc(pool_step, 1)
        pool.wait_ge(pool_step, 2)
        nc.gpsimd.affine_select(out=vision_rows[:], in_=vision_rows[:], compare_op=ALU.is_gt, fill=0.0,
                                base=SPLIT_ROW, pattern=[[0, 1]], channel_multiplier=-1).then_inc(pool_consts, 1)
        nc.gpsimd.memset(mrow[:], 0.0).then_inc(pool_consts, 1)
        nc.gpsimd.memset(zeros[:], 0.0).then_inc(pool_consts, 1)
        nc.gpsimd.memset(qa[:], 0.0).then_inc(pool_consts, 1)
        nc.gpsimd.memset(v32[:, :, :, E:32], 0.0).then_inc(pool_step, 1)
        pool.wait_ge(pool_step, 3)
        nc.gpsimd.memset(v32[:, :, :, E:E + 1], 1.0).then_inc(pool_consts, 1)
        nc.gpsimd.memset(kz[:], 0.0).then_inc(pool_step, 1)
        pool.wait_ge(pool_step, 4)
        for h in range(H):
            v = kz[:, h, :]
            nc.gpsimd.affine_select(out=v, in_=v, compare_op=ALU.not_equal, fill=-1.0,
                                    base=-((h % 2) * HR + 3 * E), pattern=[[0, NT]],
                                    channel_multiplier=1).then_inc(pool_step, 1)
            pool.wait_ge(pool_step, 5 + h)
            nc.gpsimd.affine_select(out=v, in_=v, compare_op=ALU.not_equal, fill=-1.0,
                                    base=-((h % 2) * HR + 3 * E + 1), pattern=[[0, NT]],
                                    channel_multiplier=1).then_inc(pool_consts, 1)
        with pool.Fori(0, NB * STATS) as r:
            wait_apart(pool, stat_ready, r + 1, passed)
            nc.gpsimd.tensor_scalar(vare[:], mv[:, :, 1], EPS, 1.0, ALU.add, ALU.mult).then_inc(pool_step, 1)
            pool.wait_ge(pool_step, r + 5 + H)
            nc.gpsimd.tensor_tensor(rstd[:], vare[:], half_neg[:], ALU.pow).then_inc(rstd_ready, 1)

    @block.tensor
    def _(pe):
        def transpose_tile(n, slot, banks, src):
            pe.wait_ge(xn_ready, n + 1)
            dst = ps[:, banks:banks + 2, :].rearrange("p a (c q) -> p (a c) q", q=P)
            for c in range(DC):
                last = pe.transpose(dst[:, c, :], src[:, slot, c * P:(c + 1) * P], ident[:])
            last.then_inc(tp_done, 1)

        pe.wait_ge(pool_consts, POOL_CONSTS)
        pe.wait_ge(wchunk_split, DC + 2)
        add_credits(pe, [(lo_done, 2), (v_done, 2), (qk_split, 2), (qk32_ready, 2), (s_free, 4), (exp_done, 2),
                         (pv_done, 4), (o_copied, 2), (o_norm, 1), (ot_done, 2), (oolo_done, 2), (y_done, 2), (x1_done, 1),
                         (qk_placed, 1), (m_stored, 1), (ht_stored, 1), (x1_stored, 1), (qk_stored, 1),
                         (abs_done, 1)])
        with pe.Fori(0, NB) as batch:
            b = batch
            for t in range(TT + 1):
                if t < TT:
                    pe.wait_ge(lo_done, b * (2 * TT) + t + 1)
                    transpose_tile(b * (2 * TT) + t, t % 2, 2 * (t % 2), xn)
                if t >= 1:
                    u = t - 1
                    pe.wait_ge(lo_done, b * (2 * TT) + u + 3)
                    pe.wait_ge(v_done, b * TT + u + 1)
                    k = 0
                    for a, w in ((0, 0), (1, 0), (0, 1)):
                        for c in range(DC):
                            last = pe.matmul(ps[:, 4 + u % 2, 0:HD], xt[a][:, c, u * P:(u + 1) * P],
                                             wqkv[w][:, c, 2 * HD:3 * HD], start=k == 0, stop=k == 3 * DC - 1)
                            k += 1
                    last.then_inc(v_mm, 1)
            for n in range(4):
                half, m = n // 2, n % 2
                pe.wait_ge(qk32_ready, b * 4 + n + 1)
                k = 0
                for a, w in ((0, 0), (1, 0), (0, 1)):
                    for c in range(DC):
                        last = pe.matmul(ps[:, 6 + n % 2, :], wqkv[w][:, c, m * HD:(m + 1) * HD],
                                         xt[a][:, c, half * BANK:(half + 1) * BANK],
                                         start=k == 0, stop=k == 3 * DC - 1)
                        k += 1
                last.then_inc(qk_mm, 1)
            b = again(pe, batch, "maxima")
            pe.wait_ge(qk_placed, (b + 1) * (PLACES * 16) + 1)
            pe.wait_ge(v_done, (b + 1) * TT + 2)
            pe.wait_ge(qk32_ready, (b + 1) * 4 + 2)
            for i in range(TT * H):
                qt, h = i // H, i % H
                pe.wait_ge(s_free, b * (TT * H) + i + 1)
                for k in range(HALF):
                    last = pe.matmul(ps[:, 2 * (i % 4) + k, :], qa[:, h // 2, qt * P:(qt + 1) * P],
                                     kz[:, h, k * BANK:(k + 1) * BANK], start=True, stop=True)
                last.then_inc(s_mm, 1)
            pe.wait_ge(s_free, (b + 1) * (TT * H) + 4)
            pe.transpose(ps[:, 0, 0:P], mrow[:], ident[:]).then_inc(mt_done, 1)
            pe.wait_ge(mlo_done, b + 1)
            pe.wait_ge(m_placed, (b + 1) * 64)

            b = again(pe, batch, "values")
            def scores(i):
                unit, kt, pair = i // 16, (i // 2) % TT, i % 2
                g, qh = unit // 2, unit % 2
                pe.wait_ge(exp_done, b * 64 + i + 1)
                for k in range(2):
                    h = 4 * g + 2 * pair + k
                    last = pe.matmul(ps[:, 2 * (i % 2) + k, :], kz[:, h, kt * P:(kt + 1) * P],
                                     qa[:, h // 2, qh * BANK:(qh + 1) * BANK], start=True, stop=True)
                last.then_inc(st_ready, 1)

            def values(i):
                unit, kt, pair = i // 16, (i // 2) % TT, i % 2
                g = unit // 2
                if i % 16 == 0:
                    pe.wait_ge(o_copied, b * 4 + unit + 1)
                pe.wait_ge(exp_done, b * 64 + i + 3)
                for k in range(2):
                    j = 2 * pair + k
                    last = pe.matmul(ps[32 * j:32 * (j + 1), 4 + unit % 2, :], v32[:, kt, 4 * g + j, :],
                                     p32[:, i % 4, k, :], start=kt == 0, stop=kt == TT - 1)
                last.then_inc(pv_done, 1)

            def back(unit):
                pe.wait_ge(o_copied, b * 4 + unit + 3)
                pe.wait_ge(o_norm, b * 4 + unit + 1)
                for q in range(4):
                    last = pe.transpose(ps[:, 6, q * P:(q + 1) * P], osb[:, unit % 2, q * P:(q + 1) * P], ident[:])
                last.then_inc(ot_done, 1)

            for i in range(64):
                scores(i)
                if i >= 1:
                    values(i - 1)
                if i % 16 == 4 and i > 16:
                    back(i // 16 - 1)
            values(63)
            back(3)
            b = again(pe, batch, "output")
            pe.wait_ge(o_norm, (b + 1) * 4 + 1)
            for g in range(NG):
                for u in range(GRP):
                    t = g * GRP + u
                    pe.wait_ge(oolo_done, b * TT + t + 1)
                    if t:
                        pe.wait_ge(oolo_done, b * TT + t + 2)
                    pe.transpose(ps[:, 6, 0:P], onorm[:, t, :], ident[:]).then_inc(oo_done, 1)
                    pe.wait_ge(oolo_done, b * TT + t + 3)
                    pe.wait_ge(y_done, b * TT + t + 1)
                    for k in range(2):
                        for n, (a, w) in enumerate(((0, 0), (1, 0), (0, 1))):
                            last = pe.matmul(ps[:, 2 * (t % 2) + k, :], ot[a][:, t % 2, :],
                                             wo[w][:, k * BANK:(k + 1) * BANK], start=n == 0, stop=n == 2)
                    last.then_inc(y_mm, 1)
                for u in range(GRP):
                    t = g * GRP + u
                    n = b * (2 * TT) + TT + t
                    pe.wait_ge(lo_done, n + 2)
                    transpose_tile(n, t % 2, 4, xn)
                    pe.wait_ge(lo_done, n + 3)
                    k = 0
                    for a, w in ((0, 0), (1, 0), (0, 1)):
                        for c in range(DC):
                            last = pe.matmul(ps[:, 7, t * NE:(t + 1) * NE], xt[a][:, c, t * P:(t + 1) * P],
                                             gw[w][:, c, :], start=k == 0, stop=k == 3 * DC - 1)
                            k += 1
                    last.then_inc(gate_mm, 1)
            pe.wait_ge(sums_ready, b + 1)
            pe.matmul(ps[:, 6, 0:2], ones[:], parts[:], start=True, stop=True).then_inc(sums_mm, 1)
            pe.wait_ge(gate_done, b + 1)

    @block.scalar
    def _(act):
        act.wait_ge(const_in, NCONST * 16)
        with act.Fori(0, NB) as batch:
            b = batch
            act.wait_ge(ht_stored, b * 32 + 1)

            def high(n, t, banks):
                act.wait_ge(tp_done, n + 1)
                src = ps[:, banks:banks + 2, :].rearrange("p a (c q) -> p (a c) q", q=P)
                nc.scalar.activation(xt[0][:, :, t * P:(t + 1) * P], src, ACT.Copy).then_inc(hi_done, 1)

            for t in range(TT):
                high(b * (2 * TT) + t, t, 2 * (t % 2))
            for n in range(4):
                act.wait_ge(qk_mm, b * 4 + n + 1)
                act.wait_ge(qk_split, b * 4 + n + 1)
                nc.scalar.activation(qk32[:, n % 2, :], ps[:, 6 + n % 2, :], ACT.Identity,
                                     bias=bqk[:, n % 2:n % 2 + 1], scale=1.0 / WS).then_inc(qk32_ready, 1)
            b = again(act, batch, "values")
            act.wait_ge(mt_done, b + 1)
            act.wait_ge(m_stored, b * 32 + 1)
            nc.scalar.activation(ms[0][:], ps[:, 0, 0:P], ACT.Copy).then_inc(mhi_done, 1)

            def copy_out(unit):
                act.wait_ge(pv_done, b * 64 + 16 * (unit + 1) + 4)
                act.wait_ge(ot_done, b * 4 + unit + 1)
                nc.scalar.activation(osb[:, unit % 2, :], ps[:, 4 + unit % 2, :], ACT.Copy).then_inc(o_copied, 1)

            for i in range(64):
                act.wait_ge(st_ready, b * 64 + i + 1)
                act.wait_ge(pv_done, b * 64 + i + 1)
                nc.scalar.activation(p32[:, i % 4], ps[:, 2 * (i % 2):2 * (i % 2) + 2, :], ACT.Exp
                                     ).then_inc(exp_done, 1)
                if i % 16 == 1 and i > 16:
                    copy_out(i // 16 - 1)
            copy_out(3)
            b = again(act, batch, "output")
            for g in range(NG):
                for u in range(GRP):
                    t = g * GRP + u
                    act.wait_ge(oo_done, b * TT + t + 1)
                    nc.scalar.activation(ot[0][:, t % 2, :], ps[:, 6, 0:P], ACT.Copy).then_inc(oohi_done, 1)
                for u in range(GRP):
                    t = g * GRP + u
                    n = b * (2 * TT) + TT + t
                    act.wait_ge(xn_ready, n + 1)
                    act.wait_ge(abs_done, b * TT + t + 1)
                    nc.scalar.activation(habs[:], xn[:, t % 2, :], ACT.Abs, accum_out=asum[:, t:t + 1]
                                         ).then_inc(abs_done, 1)
                    high(n, t, 4)
            act.wait_ge(lg_ready, b + 1)
            nc.scalar.activation(sc[:], lg[:], ACT.Exp).then_inc(lg_exp, 1)

    @block.vector
    def _(dve):
        def split(dst_hi, dst_lo, src):
            nc.vector.tensor_scalar(dst_hi, src, WS, None, ALU.mult).then_inc(dve_step, 1)
            count[0] += 1
            dve.wait_ge(dve_step, count[0])
            return nc.vector.scalar_tensor_tensor(out=dst_lo, in0=src, scalar=WS, in1=dst_hi, op0=ALU.mult,
                                                  op1=ALU.subtract)

        count = [0]
        dve.wait_ge(const_in, NCONST * 16)
        split(wo[0][:], wo[1][:], y4[:, 0, :]).then_inc(wchunk_split, 1)
        split(gw[0][:], gw[1][:], gstage[:]).then_inc(wchunk_split, 1)
        for c in range(DC):
            dve.wait_ge(wchunk_in, (c + 1) * 16)
            split(wqkv[0][:, c, :], wqkv[1][:, c, :], wstage[:]).then_inc(wchunk_split, 1)
        prologue_steps = count[0]
        dve.wait_ge(pool_consts, POOL_CONSTS)
        with dve.Fori(0, NB) as batch:
            b = batch
            steps = [0]

            def link(ins):
                steps[0] += 1
                ins.then_inc(dve_step, 1)
                wait_apart(dve, dve_step, b * PER_BATCH + prologue_steps + steps[0], passed)

            def tile_stats(u, src):
                for k in range(2):
                    last = nc.vector.bn_stats(stats[:, u, k, :], src[:, k * BANK:(k + 1) * BANK])
                return last

            def group_stats(last):
                link(last)
                for u in range(GRP):
                    last = nc.vector.bn_aggr(mv[:, u, :], stats[:, u].rearrange("p k s -> p (k s)"))
                last.then_inc(stat_ready, 1)
                rounds[0] += 1
                dve.wait_ge(rstd_ready, b * STATS + rounds[0])

            def normalise(dst, src, u):
                return nc.vector.tensor_scalar(dst, src, mv[:, u, 0:1], rstd[:, u:u + 1], ALU.subtract, ALU.mult)

            def low(n, t, banks):
                dve.wait_ge(hi_done, n + 1)
                src = ps[:, banks:banks + 2, :].rearrange("p a (c q) -> p (a c) q", q=P)
                nc.vector.tensor_tensor(xt[1][:, :, t * P:(t + 1) * P], src, xt[0][:, :, t * P:(t + 1) * P],
                                        ALU.subtract).then_inc(lo_done, 1)

            def value_tile(t):
                dve.wait_ge(v_mm, b * TT + t + 1)
                nc.vector.scalar_tensor_tensor(
                    out=v32[:, t, :, 0:E], in0=ps[:, 4 + t % 2, 0:HD].rearrange("p (h e) -> p h e", h=H),
                    scalar=1.0 / WS, in1=bv[:].rearrange("p (h e) -> p h e", h=H), op0=ALU.mult,
                    op1=ALU.add).then_inc(v_done, 1)

            rounds = [0]
            for g in range(NG):
                dve.wait_ge(x_landed[g], (b + 1) * 16)
                for u in range(GRP):
                    last = tile_stats(u, xin[:, g * GRP + u, :])
                group_stats(last)
                for u in range(GRP):
                    t = g * GRP + u
                    n = b * (2 * TT) + t
                    if t >= 2:
                        dve.wait_ge(tp_done, n - 1)
                    normalise(xn[:, t % 2, :], xin[:, t, :], u).then_inc(xn_ready, 1)
                    if t >= 1:
                        low(n - 1, t - 1, 2 * ((t - 1) % 2))
                    if t >= 2:
                        value_tile(t - 2)
            low(b * (2 * TT) + TT - 1, TT - 1, 2 * ((TT - 1) % 2))
            value_tile(TT - 2)
            value_tile(TT - 1)
            dve.wait_ge(qk_stored, b * 64 + 1)
            for n in range(4):
                half, m = n // 2, n % 2
                cols = slice(half * BANK, (half + 1) * BANK)
                dve.wait_ge(qk32_ready, b * 4 + n + 3)
                link(nc.vector.tensor_copy(qks[m][0][:, cols], qk32[:, n % 2, :]))
                nc.vector.tensor_tensor(qks[m][1][:, cols], qk32[:, n % 2, :], qks[m][0][:, cols],
                                        ALU.subtract).then_inc(qk_split, 1)
            b = again(dve, batch, "maxima")
            for i in range(TT * H):
                qt, h = i // H, i % H
                dve.wait_ge(s_mm, b * (TT * H) + i + 1)
                nc.vector.reduce_max(mrow[:, h * TT + qt:h * TT + qt + 1],
                                     ps[:, 2 * (i % 4):2 * (i % 4) + 2, :].rearrange("p a n -> p (a n)"),
                                     AX.X).then_inc(s_free, 1)
            dve.wait_ge(mhi_done, b + 1)
            nc.vector.tensor_tensor(ms[1][:], ps[:, 0, 0:P], ms[0][:], ALU.subtract).then_inc(mlo_done, 1)
            for unit in range(4):
                g, qh = unit // 2, unit % 2
                dve.wait_ge(ot_done, b * 4 + unit + 3)
                o4 = ps[:, 6, :].rearrange("p (q j e) -> p q j e", q=4, j=4)
                link(nc.vector.reciprocal(rinv[:], o4[:, :, :, E:E + 1]))
                for q in range(4):
                    last = nc.vector.tensor_tensor(
                        onorm[:, 4 * qh + q, 4 * E * g:4 * E * (g + 1)].rearrange("p (j e) -> p j e", j=4),
                        o4[:, q, :, 0:E], rinv[:, q].to_broadcast([P, 4, E]), ALU.mult)
                last.then_inc(o_norm, 1)
            b = again(dve, batch, "output")
            for g in range(NG):
                dve.wait_ge(x1_stored, b * (NG * 16) + g * 16 + 1)
                for u in range(GRP + 1):
                    t = g * GRP + u
                    if u < GRP:
                        dve.wait_ge(oohi_done, b * TT + t + 1)
                        nc.vector.tensor_tensor(ot[1][:, t % 2, :], ps[:, 6, 0:P], ot[0][:, t % 2, :],
                                                ALU.subtract).then_inc(oolo_done, 1)
                    if u >= 1:
                        t, v = t - 1, u - 1
                        dve.wait_ge(y_mm, b * TT + t + 1)
                        ins = nc.vector.scalar_tensor_tensor(
                            out=y4[:, v, :], in0=ps[:, 2 * (t % 2):2 * (t % 2) + 2, :].rearrange("p a n -> p (a n)"),
                            scalar=1.0 / (WS * float(HD) ** 0.5), in1=bo[:], op0=ALU.mult, op1=ALU.add)
                        ins.then_inc(y_done, 1)
                        dve.wait_ge(y_done, b * TT + t + 3)
                        last = tile_stats(v, y4[:, v, :])
                group_stats(last)
                for u in range(GRP):
                    last = normalise(y4[:, u, :], y4[:, u, :], u)
                link(last)
                for u in range(GRP):
                    nc.vector.tensor_tensor(y4[:, u, :], y4[:, u, :], xin[:, g * GRP + u, :], ALU.add
                                            ).then_inc(x1_done, 1)
                dve.wait_ge(x1_done, b * TT + (g + 1) * GRP + 1)
                for u in range(GRP):
                    last = tile_stats(u, y4[:, u, :])
                group_stats(last)
                for u in range(GRP):
                    t = g * GRP + u
                    n = b * (2 * TT) + TT + t
                    dve.wait_ge(tp_done, n - 1)
                    if t >= 2:
                        dve.wait_ge(abs_done, b * TT + t - 1 + 1)
                    normalise(xn[:, t % 2, :], y4[:, u, :], u).then_inc(xn_ready, 1)
                    if u:
                        low(n - 1, t - 1, 4)
                low(b * (2 * TT) + TT + g * GRP + GRP - 1, g * GRP + GRP - 1, 4)
            b = again(dve, batch, "gate")
            dve.wait_ge(abs_done, (b + 1) * TT + 1)
            nc.vector.reduce_sum(gs[:, 0:1], asum[:, 0:SPLIT_TILE], AX.X)
            link(nc.vector.reduce_sum(gs[:, 1:2], asum[:, SPLIT_TILE:TT], AX.X))
            link(nc.vector.tensor_tensor(gs[:, 2:3], asum[:, SPLIT_TILE:SPLIT_TILE + 1], vision_rows[:], ALU.mult))
            nc.vector.tensor_tensor(parts[:, 0:1], gs[:, 0:1], gs[:, 2:3], ALU.add)
            nc.vector.tensor_tensor(parts[:, 1:2], gs[:, 1:2], gs[:, 2:3], ALU.subtract).then_inc(sums_ready, 1)
            dve.wait_ge(sums_mm, b + 1)
            link(nc.vector.tensor_scalar(gs[:, 3:4], ps[:, 6, 0:1], 1.0 / (VISION * D), 1e-8, ALU.mult, ALU.add))
            link(nc.vector.reciprocal(gs[:, 4:5], gs[:, 3:4]))
            link(nc.vector.scalar_tensor_tensor(out=gs[:, 5:6], in0=ps[:, 6, 1:2], scalar=1.0 / ((NT - VISION) * D),
                                                in1=gs[:, 4:5], op0=ALU.mult, op1=ALU.mult))
            link(nc.vector.scalar_tensor_tensor(out=gbase[:], in0=gw_ratio[:], scalar=gs[:, 5:6], in1=gate_b[:],
                                                op0=ALU.mult, op1=ALU.add))
            dve.wait_ge(gate_mm, (b + 1) * TT)
            link(nc.vector.scalar_tensor_tensor(
                out=lg[:], in0=ps[:, 7, 0:TT * NE].rearrange("p (t e) -> p t e", e=NE), scalar=1.0 / WS,
                in1=gbase[:].unsqueeze(1).to_broadcast([P, TT, NE]), op0=ALU.mult, op1=ALU.add))
            g2 = g1[:].unsqueeze(3)
            link(nc.vector.reduce_max(g2[:, 0], lg[:], AX.X))
            nc.vector.tensor_tensor(lg[:], lg[:], g2[:, 0].to_broadcast([P, TT, NE]), ALU.subtract
                                    ).then_inc(lg_ready, 1)
            dve.wait_ge(lg_exp, b + 1)
            link(nc.vector.reduce_sum(g2[:, 1], sc[:], AX.X))
            link(nc.vector.reciprocal(g2[:, 2], g2[:, 1]))
            link(nc.vector.tensor_tensor(sc[:], sc[:], g2[:, 2].to_broadcast([P, TT, NE]), ALU.mult))
            nc.vector.reduce_max(g2[:, 3], sc[:], AX.X)
            nc.vector.tensor_tensor(g2[:, 4], sc[:, :, 0:1], sc[:, :, 1:2], ALU.min)
            link(nc.vector.tensor_tensor(g2[:, 5], sc[:, :, 0:1], sc[:, :, 1:2], ALU.max))
            link(nc.vector.tensor_tensor(g2[:, 5], g2[:, 5], sc[:, :, 2:3], ALU.min))
            link(nc.vector.tensor_tensor(g2[:, 4], g2[:, 4], g2[:, 5], ALU.max))
            link(nc.vector.scalar_tensor_tensor(out=g2[:, 6], in0=g2[:, 3], scalar=1e-8, in1=g2[:, 4],
                                                op0=ALU.add, op1=ALU.add))
            link(nc.vector.reciprocal(g2[:, 7], g2[:, 6]))
            for k in range(2):
                nc.vector.tensor_tensor(keep["tv"][:, bass.ds(b * (2 * TT) + k * TT, TT)], g1[:, 3 + k, :],
                                        g1[:, 7, :], ALU.mult)
            a, c, d = (sc[0:1, 0, k:k + 1] for k in range(NE))

            def flag(k, x, y, op):
                return nc.vector.tensor_tensor(jt[:, k:k + 1], x, y, op)

            flag(0, a, c, ALU.is_ge)
            flag(1, a, d, ALU.is_ge)
            flag(2, c, d, ALU.is_ge)
            flag(3, c, a, ALU.is_le)
            flag(4, d, a, ALU.is_le)
            link(flag(5, d, c, ALU.is_le))
            flag(6, jt[:, 0:1], jt[:, 1:2], ALU.mult)
            link(flag(7, jt[:, 4:5], jt[:, 5:6], ALU.mult))
            nc.vector.tensor_scalar(jt[:, 8:9], jt[:, 6:7], -1.0, 1.0, ALU.mult, ALU.add)
            nc.vector.tensor_scalar(jt[:, 9:10], jt[:, 2:3], -1.0, 2.0, ALU.mult, ALU.add)
            link(nc.vector.tensor_scalar(jt[:, 10:11], jt[:, 3:4], -1.0, 2.0, ALU.mult, ALU.add))
            flag(11, jt[:, 8:9], jt[:, 9:10], ALU.mult)
            link(flag(12, jt[:, 7:8], jt[:, 10:11], ALU.mult))
            link(flag(13, jt[:, 12:13], jt[:, 3:4], ALU.add))
            link(flag(14, jt[:, 11:12], jt[:, 13:14], ALU.add))
            nc.vector.tensor_copy(keep["jobs"][:, bass.ds(b * 2, 1)], jt[:, 11:12])
            nc.vector.tensor_scalar(keep["jobs"][:, bass.ds(b * 2 + 1, 1)], jt[:, 14:15], -1.0, 3.0, ALU.mult,
                                    ALU.add).then_inc(gate_done, 1)
            assert steps[0] == PER_BATCH, steps[0]


PER_BATCH = 38


def expert_phase(nc, io, scr, keep, out, ctx):

    def sb(name, shape, dt=F32):
        return ctx.enter_context(nc.sbuf_tensor(name, shape, dt))

    def sem(name):
        return ctx.enter_context(nc.semaphore(name))

    ps1 = ctx.enter_context(nc.psum_tensor("ps1", [P, 2, NT], F32))
    ps2 = ctx.enter_context(nc.psum_tensor("ps2", [P, 2, D], F32))
    JOBS = 2 * NB

    stage = sb("stage", [P, STAGE, D])
    w1 = [sb(f"w1{i}", [P, DC, D], F16) for i in range(2)]
    w2 = [sb(f"w2{i}", [P, DC, D], F16) for i in range(2)]
    ht = [sb(f"ht{i}", [P, DC, NT], F16) for i in range(2)]
    hid = [sb(f"hid{i}", [P, DC, NT], F16) for i in range(2)]
    act32 = sb("act32", [P, 2, NT])
    b2bc = sb("b2bc", [P, D])
    etmp = sb("etmp", [P, 2, D])
    moe = sb("moe", [P, TT, D])
    x1b = sb("x1b", [P, 2, D])
    stats = sb("stats2", [P, TT, 2, 6])
    mv = sb("mv2", [P, TT, 2])
    std = sb("std2", [P, TT])
    rstd = sb("rstd2", [P, TT])
    epsc = sb("epsc", [P, 1])

    stage_landed = [sem(f"stage_landed{i}") for i in range(STAGE)]
    chunk_split = sem("chunk_split")
    pool_step2 = sem("pool_step2")
    ht_landed = sem("ht_landed")
    b2_landed = sem("b2_landed")
    mm1_done = sem("mm1_done")
    mm2_done = sem("mm2_done")
    act_done = sem("act_done")
    hidden_hi = sem("hidden_hi")
    hidden_split = sem("hidden_split")
    evac_done = sem("evac_done")
    etmp_done = sem("etmp_done")
    eps_ready = sem("eps_ready")
    var_ready = sem("var_ready")
    std_ready = sem("std_ready")
    dve_step2 = sem("dve_step2")
    x1_landed = [sem(f"x1_landed{i}") for i in range(2)]
    norm_done = sem("norm_done")
    y_ready = sem("y_ready")
    y_stored = sem("y_stored")
    passed2 = sem("passed2")

    w_dram = (io["w1"].rearrange("e (c p) n -> e c p n", p=P), io["w2"].rearrange("e (c p) n -> e c p n", p=P))
    out_v = out.rearrange("b (t p) d -> (b t) p d", p=P)
    x1_v = scr["x1"].rearrange("b (t p) d -> (b t) p d", p=P)
    block = ctx.enter_context(nc.Block())

    @block.sync
    def _(sp):
        with sp.Fori(0, NB) as b:
            for s in range(2):
                e = sp.value_load(keep["jobs"][:, bass.ds(b * 2 + s, 1)], min_val=0, max_val=NE - 1)
                if s == 0:
                    sp.wait_ge(mm1_done, b * (2 * TT) + 1)
                    for i in range(2):
                        sp.dma_start(ht[i][:], scr["ht"][i][bass.ds(b, 1)].rearrange("o p c t -> (o p) c t")
                                     ).then_inc(ht_landed, 16)
                for which in range(2):
                    for c in range(DC):
                        k = which * DC + c
                        sp.wait_ge(chunk_split, b * (4 * DC) + (s * 2 * DC + k + 1))
                        sp.dma_start(stage[:, k % STAGE, :],
                                     w_dram[which][bass.ds(e, 1), c].rearrange("o p n -> (o p) n")
                                     ).then_inc(stage_landed[k % STAGE], 16)
                sp.wait_ge(evac_done, b * (2 * TT) + s * TT + 2)
                sp.dma_start(b2bc[:], io["b2"][bass.ds(e, 1)].to_broadcast([P, D])).then_inc(b2_landed, 16)

    @block.gpsimd
    def _(pool):
        add_credits(pool, [(chunk_split, STAGE), (act_done, 2), (hidden_split, 2), (evac_done, 2),
                           (mm1_done, 1), (mm2_done, 1), (y_ready, 1), (y_stored, 1)])
        with pool.Fori(0, JOBS) as job:
            for which in range(2):
                w = (w1, w2)[which]
                pool.wait_ge((mm1_done, mm2_done)[which], job * TT + 1)
                for c in range(DC):
                    k = which * DC + c
                    src = stage[:, k % STAGE, :]
                    wait_apart(pool, stage_landed[k % STAGE], job * (2 * DC // STAGE * 16) + (k // STAGE + 1) * 16,
                               passed2)
                    nc.gpsimd.tensor_scalar(w[0][:, c, :], src, WS, 1.0, ALU.mult, ALU.mult).then_inc(pool_step2, 1)
                    wait_apart(pool, pool_step2, job * (4 * DC) + 2 * k + 1, passed2)
                    nc.gpsimd.tensor_scalar(src, src, WS, 1.0, ALU.mult, ALU.mult).then_inc(pool_step2, 1)
                    pool.wait_ge(pool_step2, job * (4 * DC) + 2 * k + 2)
                    nc.gpsimd.tensor_tensor(w[1][:, c, :], src, w[0][:, c, :], ALU.subtract).then_inc(chunk_split, 1)

    @block.tensor
    def _(pe):
        with pe.Fori(0, NB) as b:
            for s in range(2):
                if s == 0:
                    pe.wait_ge(ht_landed, (b + 1) * 32)
                wait_apart(pe, chunk_split, b * (4 * DC) + (s * 2 * DC + DC + STAGE), passed2)
                with pe.Fori(0, TT // 2) as pair:
                    f0 = pair * 2
                    for u in range(2):
                        pe.wait_ge(act_done, b * (2 * TT) + f0 + (s * TT + u + 1))
                        for half in range(HALF):
                            k = 0
                            for a, w in ((0, 0), (1, 0), (0, 1)):
                                for c in range(DC):
                                    last = pe.matmul(ps1[:, u, half * BANK:(half + 1) * BANK],
                                                     w1[w][:, c, bass.ds(f0 * P + u * P, P)],
                                                     ht[a][:, c, half * BANK:(half + 1) * BANK],
                                                     start=k == 0, stop=k == 3 * DC - 1)
                                    k += 1
                        last.then_inc(mm1_done, 1)
                pe.wait_ge(chunk_split, b * (4 * DC) + ((s + 1) * 2 * DC + STAGE))
                wait_apart(pe, hidden_split, b * (2 * TT) + ((s + 1) * TT + 2), passed2)
                with pe.Fori(0, TT // 2) as pair:
                    t0 = pair * 2
                    for u in range(2):
                        pe.wait_ge(evac_done, b * (2 * TT) + t0 + (s * TT + u + 1))
                        for half in range(HALF):
                            k = 0
                            for a, w in ((0, 0), (1, 0), (0, 1)):
                                for c in range(DC):
                                    last = pe.matmul(ps2[:, u, half * BANK:(half + 1) * BANK],
                                                     hid[a][:, c, bass.ds(t0 * P + u * P, P)],
                                                     w2[w][:, c, half * BANK:(half + 1) * BANK],
                                                     start=k == 0, stop=k == 3 * DC - 1)
                                    k += 1
                        last.then_inc(mm2_done, 1)

    @block.scalar
    def _(act):
        def hidden_tiles(b, s, e, func):
            with act.Fori(0, TT // 2) as pair:
                f0 = pair * 2
                for u in range(2):
                    act.wait_ge(mm1_done, b * (2 * TT) + f0 + (s * TT + u + 1) + 1)
                    act.wait_ge(hidden_split, b * (2 * TT) + f0 + (s * TT + u + 1))
                    nc.scalar.activation(act32[:, u, :], ps1[:, u, :], func,
                                         bias=keep["b1"][:, bass.ds(f0 + (e * DC + u), 1)], scale=1.0 / WS
                                         ).then_inc(act_done, 1)

        act.wait_ge(eps_ready, 1)
        with act.Fori(0, NB) as b:
            for s in range(2):
                j = act.value_load(keep["jobs"][:, bass.ds(b * 2 + s, 1)], min_val=0, max_val=NE - 1)
                for e, func in enumerate((ACT.Tanh, ACT.Gelu, ACT.Silu)):
                    with act.If(j == e):
                        hidden_tiles(b, s, e, func)
            act.wait_ge(var_ready, b + 1)
            nc.scalar.activation(std[:], mv[:, :, 1], ACT.Sqrt, bias=epsc[:]).then_inc(std_ready, 1)
            for t in range(TT):
                if t == 0:
                    act.wait_ge(y_ready, b * TT + 1)
                    for k in range(2):
                        act.dma_start(x1b[:, k, :], x1_v[bass.ds(b * TT + k, 1)].rearrange("o p d -> (o p) d")
                                      ).then_inc(x1_landed[k], 16)
                act.wait_ge(y_ready, b * TT + t + 2)
                act.dma_start(out_v[bass.ds(b * TT + t, 1)].rearrange("o p d -> (o p) d"), moe[:, t, :]
                              ).then_inc(y_stored, 16)
                if t + 2 < TT:
                    act.dma_start(x1b[:, t % 2, :], x1_v[bass.ds(b * TT + t + 2, 1)].rearrange("o p d -> (o p) d")
                                  ).then_inc(x1_landed[t % 2], 16)
        act.wait_ge(y_stored, NB * TT * 16 + 1)

    @block.vector
    def _(dve):
        nc.vector.memset(epsc[:], EPS).then_inc(eps_ready, 1)
        with dve.Fori(0, NB) as b:
            for s in range(2):
                wait_apart(dve, mm2_done, b * (2 * TT) + s * TT + 1, passed2)
                with dve.Fori(0, TT // 2) as pair:
                    f0 = pair * 2
                    for u in range(2):
                        n = b * (2 * TT) + f0 + (s * TT + u)
                        dve.wait_ge(act_done, n + 3)
                        nc.vector.tensor_copy(hid[0][:, bass.ds(f0 + u, 1), :].rearrange("p o n -> p (o n)"),
                                              act32[:, u, :]).then_inc(hidden_hi, 1)
                        dve.wait_ge(hidden_hi, n + 1)
                        nc.vector.tensor_tensor(hid[1][:, bass.ds(f0 + u, 1), :].rearrange("p o n -> p (o n)"),
                                                act32[:, u, :],
                                                hid[0][:, bass.ds(f0 + u, 1), :].rearrange("p o n -> p (o n)"),
                                                ALU.subtract).then_inc(hidden_split, 1)
                wait_apart(dve, b2_landed, b * 32 + (s + 1) * 16, passed2)
                if s == 0:
                    wait_apart(dve, y_stored, b * (TT * 16) + 1, passed2)
                with dve.Fori(0, TT // 2) as pair:
                    t0 = pair * 2
                    for u in range(2):
                        n = b * (2 * TT) + t0 + (s * TT + u)
                        m = moe[:, bass.ds(t0 + u, 1), :].rearrange("p o n -> p (o n)")
                        tv = keep["tv"][:, bass.ds(b * (2 * TT) + t0 + (s * TT + u), 1)]
                        dve.wait_ge(mm2_done, n + 2)
                        nc.vector.scalar_tensor_tensor(out=etmp[:, u, :], in0=ps2[:, u, :], scalar=1.0 / WS,
                                                       in1=b2bc[:], op0=ALU.mult, op1=ALU.add
                                                       ).then_inc(evac_done, 1)
                        dve.wait_ge(evac_done, n + 3)
                        if s == 0:
                            nc.vector.tensor_scalar(m, etmp[:, u, :], tv, None, ALU.mult).then_inc(etmp_done, 1)
                        else:
                            nc.vector.scalar_tensor_tensor(out=m, in0=etmp[:, u, :], scalar=tv, in1=m,
                                                           op0=ALU.mult, op1=ALU.add).then_inc(etmp_done, 1)
            dve.wait_ge(etmp_done, (b + 1) * (2 * TT))
            for t in range(TT):
                for k in range(2):
                    last = nc.vector.bn_stats(stats[:, t, k, :], moe[:, t, k * BANK:(k + 1) * BANK])
            last.then_inc(dve_step2, 1)
            wait_apart(dve, dve_step2, b * 2 + 1, passed2)
            for t in range(TT):
                last = nc.vector.bn_aggr(mv[:, t, :], stats[:, t].rearrange("p k s -> p (k s)"))
            last.then_inc(var_ready, 1)
            dve.wait_ge(std_ready, b + 1)
            nc.vector.reciprocal(rstd[:], std[:]).then_inc(dve_step2, 1)
            dve.wait_ge(dve_step2, b * 2 + 2)
            for t in range(TT):
                nc.vector.tensor_scalar(moe[:, t, :], moe[:, t, :], mv[:, t, 0:1], rstd[:, t:t + 1], ALU.subtract,
                                        ALU.mult).then_inc(norm_done, 1)
                dve.wait_ge(norm_done, b * TT + t + 1)
                dve.wait_ge(x1_landed[t % 2], b * (TT // 2 * 16) + (t // 2 + 1) * 16)
                nc.vector.tensor_tensor(moe[:, t, :], moe[:, t, :], x1b[:, t % 2, :], ALU.add).then_inc(y_ready, 1)


def sandwich_block(nc, io, out):
    with ExitStack() as ctx:
        keep = {
            "tv": ctx.enter_context(nc.sbuf_tensor("tv", [P, NB * 2 * TT], F32)),
            "jobs": ctx.enter_context(nc.sbuf_tensor("jobs", [1, NB * 2], I32)),
            "b1": ctx.enter_context(nc.sbuf_tensor("b1", [P, NE * DC], F32)),
        }
        scr = {
            "qk": nc.dram_tensor("scr_qk", (2, 2, HD, NT), F16).ap(),
            "m": nc.dram_tensor("scr_m", (2, H * TT, P), F16).ap(),
            "x1": nc.dram_tensor("scr_x1", (NB, NT, D), F32).ap(),
            "ht": [nc.dram_tensor(f"scr_ht{i}", (NB, P, DC, NT), F16).ap() for i in range(2)],
        }
        with ExitStack() as phase:
            attention_phase(nc, io, scr, keep, phase)
        with ExitStack() as phase:
            expert_phase(nc, io, scr, keep, out, phase)


def kernel(**inputs):
    import numpy as np
    import concourse.bacc as bacc
    from concourse import mybir as mb
    from concourse.bass_utils import run_bass_kernel_spmd

    a = {k[3:]: np.asarray(v) for k, v in inputs.items()}
    wqk = a["attn_Wqk_w"].reshape(HD, 2, D).transpose(1, 0, 2).reshape(2 * HD, D)
    arrays = {
        "x": a["attn_x"],
        "wqkv_t": np.concatenate([wqk, a["attn_Wv_w"]], 0).T,
        "bqk": a["attn_Wqk_b"].reshape(HD, 2),
        "bv": a["attn_Wv_b"],
        "wo_t": a["attn_Wo_w"].T,
        "bo": a["attn_Wo_b"],
        "gate_w": a["ffn_gate_w"][:D],
        "gw_ratio": a["ffn_gate_w"][D],
        "gate_b": a["ffn_gate_b"],
        "w1": a["ffn_w1"],
        "b1": a["ffn_b1"].reshape(NE, DC, P).transpose(2, 0, 1).reshape(P, NE * DC),
        "w2": a["ffn_w2"],
        "b2": a["ffn_b2"],
    }
    arrays = {k: np.ascontiguousarray(v) for k, v in arrays.items()}
    nc = bacc.Bacc("TRN2", target_bir_lowering=False, num_devices=1)
    io = {k: nc.dram_tensor(f"in_{k}", v.shape, mb.dt.from_np(v.dtype), kind="ExternalInput").ap()
          for k, v in arrays.items()}
    out = nc.dram_tensor("out", (NB, NT, D), mb.dt.float32, kind="ExternalOutput").ap()
    sandwich_block(nc, io, out)
    r = run_bass_kernel_spmd(nc, [{f"in_{k}": v for k, v in arrays.items()}], core_ids=[0])
    return r.results[0]["out"]
```

```python
from contextlib import ExitStack

import concourse.bass as bass
from concourse import mybir

ALU = mybir.AluOpType
ACT = mybir.ActivationFunctionType
AX = mybir.AxisListType
F32 = mybir.dt.float32
F16 = mybir.dt.float16
I32 = mybir.dt.int32

P = 128
NB, NT, D = 4, 1024, 1024
TT = NT // P
DC = D // P
H, E = 8, 16
HD = H * E
HP = H // 2
HR = P // 2
NE = 3
BANK = 512
HALF = NT // BANK
GRP = 4
NG = TT // GRP
VISION = int(NT * 0.3)
SPLIT_TILE, SPLIT_ROW = VISION // P, VISION % P
EPS = 1e-5
WS = 64.0
STAGE = 4


def add_credits(eng, pairs):
    for sem, n in pairs:
        eng.sem_inc(sem, n)


def wait_apart(eng, sem, value, passed):
    eng.wait_ge(sem, value)
    eng.sem_inc(passed, 1)


class Batch:

    def __init__(self, reg, off=0):
        self.reg, self.off = reg, off

    def next(self):
        return Batch(self.reg, self.off + 1)

    def n(self, per_batch, i=0):
        fixed = self.off * per_batch + i
        return fixed if self.reg is None else self.reg * per_batch + fixed

    def again(self, eng, stage):
        if self.reg is None:
            return self
        with eng.register(f"batch_{stage}") as reg:
            eng.reg_mov(reg, self.reg)
            return Batch(eng.snap(reg, min_val=0, max_val=NB - 2), self.off)


def split_weights(nc, pool, w, c, src, step, steps_before, wait):
    nc.gpsimd.tensor_scalar(w[0][:, c, :], src, WS, 1.0, ALU.mult, ALU.mult).then_inc(step, 1)
    wait(step, steps_before + 1)
    nc.gpsimd.tensor_scalar(src, src, WS, 1.0, ALU.mult, ALU.mult).then_inc(step, 1)
    pool.wait_ge(step, steps_before + 2)
    return nc.gpsimd.tensor_tensor(w[1][:, c, :], src, w[0][:, c, :], ALU.subtract)


def attention_phase(nc, io, scr, keep, ctx):

    def sb(name, shape, dt=F32):
        return ctx.enter_context(nc.sbuf_tensor(name, shape, dt))

    def sem(name):
        return ctx.enter_context(nc.semaphore(name))

    ps = ctx.enter_context(nc.psum_tensor("ps", [P, 8, BANK], F32))
    WIDE = (0, 2)
    NARROW = (6, 7)
    ST = (0, 2)
    O_BANK, OT_BANK = 4, 5
    FRONT_TP = 6
    Y, TAIL_TP = 0, 2
    QKV = (4, 5)
    OO_BANK, GATE_BANK = 6, 7

    ident = sb("ident", [P, P])
    ones = sb("ones", [P, P])
    vision_rows = sb("vision_rows", [P, 1])
    half_neg = sb("half_neg", [P, GRP])
    eps4 = sb("eps4", [P, GRP])
    wstage = sb("wstage", [P, 3 * HD])
    gstage = sb("gstage", [P, DC, NE])
    wqkv = [sb(f"wqkv{i}", [P, DC, 3 * HD], F16) for i in range(2)]
    wo = [sb(f"wo{i}", [P, D], F16) for i in range(2)]
    gw = [sb(f"gw{i}", [P, DC, NE], F16) for i in range(2)]
    bqk = sb("bqk", [P, 2])
    bv = sb("bv", [P, HD])
    bo = sb("bo", [P, D])
    gw_ratio = sb("gw_ratio", [P, NE])
    gate_b = sb("gate_b", [P, NE])
    xa = keep["ring"]
    xres = sb("xres", [P, GRP, D])
    xn = sb("xn", [P, 2, D])
    xt = keep["wide16"]
    ht = [sb(f"hta{i}", [P, DC, GRP * P], F16) for i in range(2)]
    qk32 = sb("qk32", [P, 2, BANK])
    qks = [[sb(f"qks{m}{i}", [P, NT], F16) for i in range(2)] for m in range(2)]
    qa = sb("qa", [P, HP, NT], F16)
    kz = keep["kz"]
    v32 = sb("v32", [P, TT, H, 32])
    mrow = sb("mrow", [P, 2, P])
    mpart = sb("mpart", [P, 32, 2])
    ms = [sb(f"ms{i}", [P, 2, P], F16) for i in range(2)]
    p32 = sb("p32", [P, 4, 2, BANK])
    osb = sb("osb", [P, 2, BANK])
    rinv = sb("rinv", [P, 4, 4, 1])
    onorm = sb("onorm", [P, TT, HD])
    ot = [sb(f"ot{i}", [P, 2, P], F16) for i in range(2)]
    y4 = sb("y4", [P, GRP, D])
    stats = sb("stats", [P, GRP, 2, 6])
    mv = sb("mv", [P, GRP, 2])
    vare = sb("vare", [P, GRP])
    rstd = sb("rstd", [P, GRP])
    habs = sb("habs", [P, D])
    asum = sb("asum", [P, TT])
    parts = sb("parts", [P, 2])
    gs = sb("gs", [P, 8])
    gbase = sb("gbase", [P, NE])
    lg = sb("lg", [P, TT, NE])
    sc = sb("sc", [P, TT, NE])
    g1 = sb("g1", [P, 8, TT])
    jt = sb("jt", [1, 16])

    const_in = sem("const_in")
    wchunk_in = sem("wchunk_in")
    wchunk_split = sem("wchunk_split")
    pool_consts = sem("pool_consts")
    xa_landed = [sem(f"xa_landed{k}") for k in range(GRP)]
    xres_landed = [sem(f"xres_landed{k}") for k in range(GRP)]
    dve_step = sem("dve_step")
    stat_ready = sem("stat_ready")
    pool_step = sem("pool_step")
    rstd_ready = sem("rstd_ready")
    front_norm = sem("front_norm")
    front_tp = sem("front_tp")
    front_hi = sem("front_hi")
    front_lo = sem("front_lo")
    v_mm = sem("v_mm")
    v_done = sem("v_done")
    qk_mm = sem("qk_mm")
    qk32_ready = sem("qk32_ready")
    qk_split = sem("qk_split")
    qk_stored = sem("qk_stored")
    qk_placed = sem("qk_placed")
    wide_mm = sem("wide_mm")
    wide_free = sem("wide_free")
    narrow_mm = sem("narrow_mm")
    narrow_free = sem("narrow_free")
    m_ready = sem("m_ready")
    mt_done = sem("mt_done")
    mhi_done = sem("mhi_done")
    mlo_done = sem("mlo_done")
    m_stored = sem("m_stored")
    m_placed = sem("m_placed")
    st_ready = sem("st_ready")
    exp_done = sem("exp_done")
    pv_done = sem("pv_done")
    o_copied = sem("o_copied")
    ot_done = sem("ot_done")
    o_norm = sem("o_norm")
    oo_done = sem("oo_done")
    oohi_done = sem("oohi_done")
    oolo_done = sem("oolo_done")
    y_mm = sem("y_mm")
    y_done = sem("y_done")
    x1_done = sem("x1_done")
    x1_stored = sem("x1_stored")
    tail_norm = sem("tail_norm")
    tail_tp = sem("tail_tp")
    tail_hi = sem("tail_hi")
    tail_lo = sem("tail_lo")
    ht_stored = sem("ht_stored")
    abs_done = sem("abs_done")
    gate_mm = sem("gate_mm")
    sums_ready = sem("sums_ready")
    sums_mm = sem("sums_mm")
    lg_ready = sem("lg_ready")
    lg_exp = sem("lg_exp")
    gate_done = sem("gate_done")
    passed = sem("passed")
    ring_landed = [sem(f"ring_landed{k}") for k in range(STAGE)]
    split_step = sem("split_step")
    ring_split = sem("ring_split")
    h0_landed = sem("h0_landed")
    credits = [(front_norm, GRP), (front_tp, 2), (front_lo, 1), (qk_split, 2), (qk_stored, 1), (qk_placed, 1),
               (wide_free, 2), (narrow_free, 2), (mt_done, 1), (m_stored, 1), (m_placed, 1), (exp_done, 2),
               (pv_done, 4), (o_copied, 1), (ot_done, 2), (o_norm, 1), (oolo_done, 1), (y_done, 1),
               (x1_done, GRP), (x1_stored, 1), (tail_tp, 2), (tail_lo, 1), (ht_stored, 1), (abs_done, 2),
               (gate_done, 1)]

    x_v = io["x"].rearrange("b (t p) d -> b p t d", p=P)
    x1_v = scr["x1"].rearrange("b (t p) d -> b p t d", p=P)
    wqkv_v = io["wqkv_t"].rearrange("(c p) n -> c p n", p=P)
    NCONST = 8
    POOL_CONSTS = 8 + H
    PLACES = 14
    STATS = 6
    PAIRS = 64
    NARROW_BY = 54

    FRONT_AT = {38: 0, 41: 1, 44: 2, 47: 3, 53: 4, 56: 5, 59: 6, 62: 7}
    BACK_AT = {20: 0, 36: 1, 52: 2}

    def one(ap, batch):
        return ap[bass.ds(batch.n(1), 1)].rearrange("o p t d -> (o p) t d")

    def round_of(batch, front, k, ahead=True):
        if front:
            return batch.n(STATS, k - STATS + 2) if batch.reg is not None or batch.off else k
        return batch.n(STATS, 2 + (2 if ahead else 0) + k)

    block = ctx.enter_context(nc.Block())

    def each_batch(eng, front, iteration):
        front(Batch(None, 0))
        with eng.Fori(0, NB - 1) as b:
            iteration(Batch(b), True)
        iteration(Batch(None, NB - 1), False)

    @block.sync
    def _(sp):
        def load_front(batch, tiles):
            for t in tiles:
                sp.wait_ge(front_norm, batch.n(TT, t + 1))
                sp.dma_start(xa[:, t % GRP, :], one(x_v, batch)[:, t, :]).then_inc(xa_landed[t % GRP], 16)

        def load_residual(batch, tiles):
            for t in tiles:
                sp.wait_ge(x1_done, batch.n(TT, t + 1))
                sp.dma_start(xres[:, t % GRP, :], one(x_v, batch)[:, t, :]).then_inc(xres_landed[t % GRP], 16)

        def place_qk(batch):
            sp.wait_ge(qk_placed, batch.n(PLACES * 16, 1))
            sp.wait_ge(qk_split, batch.n(4, 4 + 2))
            for m in range(2):
                for i in range(2):
                    sp.dma_start(scr["qk"][m, i], qks[m][i][:]).then_inc(qk_stored, 16)
            wait_apart(sp, qk_stored, batch.n(64, 64 + 1), passed)
            if batch.reg is not None:
                sp.wait_ge(pv_done, batch.n(PAIRS, 4))
            else:
                sp.wait_ge(pool_consts, POOL_CONSTS)
            for j in range(2):
                for slot in range(3):
                    r = j * HR + slot * E
                    qpart, kpart = slot % 2, slot // 2
                    src = scr["qk"].rearrange("m i (hp j e) t -> m i j e hp t", hp=HP, j=2)
                    sp.dma_start(qa[r:r + E], src[0, qpart, j]).then_inc(qk_placed, 16)
                    kdst = kz[r:r + E].rearrange("e (hp j) t -> e j hp t", j=2)[:, j]
                    sp.dma_start(kdst, src[1, kpart, j]).then_inc(qk_placed, 16)
                r = j * HR + 3 * E
                sp.dma_start(qa[r:r + 2], kz[3 * E + 4:3 * E + 6, 0:HP, :]).then_inc(qk_placed, 16)

        def place_maxima(batch, g):
            wait_apart(sp, m_placed, batch.n(128, 1), passed)
            sp.wait_ge(mlo_done, batch.n(2, g + 1))
            for i in range(2):
                sp.dma_start(scr["m"][g, i], ms[i][0:32, g, :]).then_inc(m_stored, 16)
            sp.wait_ge(m_stored, batch.n(64, 32 * (g + 1) + 1))
            for i in range(2):
                for j in range(2):
                    r = j * HR + 3 * E + i
                    src = scr["m"].rearrange("g i (hp j q) n -> g i j hp (q n)", hp=2, j=2)[g, i, j]
                    sp.dma_start(qa[r:r + 1, 2 * g:2 * g + 2], src.unsqueeze(0)).then_inc(m_placed, 16)

        def store_x1(batch, g):
            sp.wait_ge(x1_done, batch.n(TT, (g + 1) * GRP + GRP))
            sp.dma_start(one(x1_v, batch)[:, g * GRP:(g + 1) * GRP, :], y4[:]).then_inc(x1_stored, 16)

        def store_ht(batch, g):
            wait_apart(sp, tail_lo, batch.n(TT, (g + 1) * GRP + 1), passed)
            for i in range(2):
                sp.dma_start(one(scr["ht"][i], batch)[:, :, g * GRP * P:(g + 1) * GRP * P], ht[i][:]
                             ).then_inc(ht_stored, 16)

        def load_expert(chunks):
            if chunks[0] == 0:
                sp.wait_ge(gate_done, 1 + 1)
                sp.wait_ge(front_norm, NB * TT + GRP)
            e = sp.value_load(keep["jobs"][:, 0:1], min_val=0, max_val=NE - 1)
            for c in chunks:
                if c >= STAGE:
                    sp.wait_ge(ring_split, c - STAGE + 1)
                sp.dma_start(xa[:, c % STAGE, :], io["w1"].rearrange("e (c p) n -> e c p n", p=P)[bass.ds(e, 1), c]
                             .rearrange("o p n -> (o p) n")).then_inc(ring_landed[c % STAGE], 16)

        def front(batch):
            load_front(batch, range(GRP))
            sp.dma_start(bqk[:], io["bqk"]).then_inc(const_in, 16)
            sp.dma_start(bv[:], io["bv"].partition_broadcast(P)).then_inc(const_in, 16)
            sp.dma_start(bo[:], io["bo"].partition_broadcast(P)).then_inc(const_in, 16)
            sp.dma_start(gw_ratio[:], io["gw_ratio"].partition_broadcast(P)).then_inc(const_in, 16)
            sp.dma_start(gate_b[:], io["gate_b"].partition_broadcast(P)).then_inc(const_in, 16)
            sp.dma_start(gstage[:], io["gate_w"].rearrange("(c p) e -> p c e", p=P)).then_inc(const_in, 16)
            sp.dma_start(y4[:, 0, :], io["wo_t"]).then_inc(const_in, 16)
            sp.dma_start(keep["b1"][:], io["b1"]).then_inc(const_in, 16)
            load_front(batch, range(GRP, TT))
            for c in range(DC):
                if c:
                    sp.wait_ge(wchunk_split, c + 2)
                sp.dma_start(wstage[:], wqkv_v[c]).then_inc(wchunk_in, 16)
            place_qk(batch)

        def iteration(b, ahead):
            load_residual(b, range(GRP))
            if ahead:
                load_front(b.next(), range(GRP))
            else:
                load_expert(range(STAGE))
            for g in range(2):
                place_maxima(b, g)
                if g == 0 and not ahead:
                    load_expert(range(STAGE, DC))
            if ahead:
                load_front(b.next(), range(GRP, TT))
            load_residual(b, range(GRP, TT))
            if not ahead:
                sp.wait_ge(ht_stored, 64 + 1)
                sp.wait_ge(pv_done, NB * PAIRS + 4)
                sp.dma_start(kz[:], scr["ht"][0][0]).then_inc(h0_landed, 16)
            store_x1(b, 0)
            if ahead:
                place_qk(b.next())
            store_ht(b, 0)
            store_x1(b, 1)
            store_ht(b, 1)

        each_batch(sp, front, iteration)
        sp.wait_ge(ht_stored, NB * 64 + 1)
        sp.wait_ge(x1_stored, NB * NG * 16 + 1)
        sp.wait_ge(h0_landed, 16)

    @block.gpsimd
    def _(pool):
        add_credits(pool, credits)
        nc.gpsimd.memset(ident[:], 0.0).then_inc(pool_step, 1)
        pool.wait_ge(pool_step, 1)
        nc.gpsimd.affine_select(out=ident[:], in_=ident[:], compare_op=ALU.not_equal, fill=1.0, base=0,
                                pattern=[[-1, P]], channel_multiplier=1).then_inc(pool_consts, 1)
        nc.gpsimd.memset(half_neg[:], -0.5).then_inc(pool_consts, 1)

        def rounds(first, count, steps):
            with pool.Fori(first, first + count) as r:
                pool.wait_ge(stat_ready, r + 1)
                nc.gpsimd.tensor_tensor(vare[:], mv[:, :, 1], eps4[:], ALU.add).then_inc(pool_step, 1)
                pool.wait_ge(pool_step, r + steps + 1)
                nc.gpsimd.tensor_tensor(rstd[:], vare[:], half_neg[:], ALU.pow).then_inc(rstd_ready, 1)

        nc.gpsimd.memset(eps4[:], EPS).then_inc(pool_consts, 1)
        pool.wait_ge(pool_consts, 3)
        rounds(0, 2, 1)
        nc.gpsimd.memset(ones[:], 1.0).then_inc(pool_consts, 1)
        nc.gpsimd.memset(vision_rows[:], 1.0).then_inc(pool_step, 1)
        pool.wait_ge(pool_step, 2 + 2)
        nc.gpsimd.affine_select(out=vision_rows[:], in_=vision_rows[:], compare_op=ALU.is_gt, fill=0.0,
                                base=SPLIT_ROW, pattern=[[0, 1]], channel_multiplier=-1).then_inc(pool_consts, 1)
        nc.gpsimd.memset(mrow[:], 0.0).then_inc(pool_consts, 1)
        nc.gpsimd.memset(qa[:], 0.0).then_inc(pool_consts, 1)
        nc.gpsimd.memset(v32[:, :, :, E:32], 0.0).then_inc(pool_step, 1)
        pool.wait_ge(pool_step, 3 + 2)
        nc.gpsimd.memset(v32[:, :, :, E:E + 1], 1.0).then_inc(pool_consts, 1)
        nc.gpsimd.memset(kz[:], 0.0).then_inc(pool_step, 1)
        pool.wait_ge(pool_step, 4 + 2)
        for h in range(H):
            v = kz[:, h, :]
            nc.gpsimd.affine_select(out=v, in_=v, compare_op=ALU.not_equal, fill=-1.0,
                                    base=-((h % 2) * HR + 3 * E), pattern=[[0, NT]],
                                    channel_multiplier=1).then_inc(pool_step, 1)
            pool.wait_ge(pool_step, 5 + 2 + h)
            nc.gpsimd.affine_select(out=v, in_=v, compare_op=ALU.not_equal, fill=-1.0,
                                    base=-((h % 2) * HR + 3 * E + 1), pattern=[[0, NT]],
                                    channel_multiplier=1).then_inc(pool_consts, 1)
        rounds(2, NB * STATS - 6, 4 + H)
        pool.wait_ge(v_mm, NB * TT)
        for c in range(DC):
            pool.wait_ge(ring_landed[c % STAGE], (c // STAGE + 1) * 16)
            split_weights(nc, pool, xt, c, xa[:, c % STAGE, :], split_step, 2 * c, pool.wait_ge
                          ).then_inc(ring_split, 1)
        rounds(NB * STATS - 4, 4, 4 + H)

    THREE = ((0, 0), (1, 0), (0, 1))

    @block.tensor
    def _(pe):
        def transpose_tile(slot, banks):
            dst = ps[:, banks:banks + 2, :].rearrange("p a (c q) -> p (a c) q", q=P)
            for c in range(DC):
                last = pe.transpose(dst[:, c, :], xn[:, slot, c * P:(c + 1) * P], ident[:])
            return last

        def front_tile(batch, t):
            pe.wait_ge(front_norm, batch.n(TT, t + 1 + GRP))
            pe.wait_ge(front_lo, batch.n(TT, t + 1))
            transpose_tile(t % 2, FRONT_TP).then_inc(front_tp, 1)

        def qk_unit(batch, n):
            half, m = n // 2, n % 2
            if n >= 2:
                pe.wait_ge(qk32_ready, batch.n(4, n - 1))
            k = 0
            for a, w in THREE:
                for c in range(DC):
                    last = pe.matmul(ps[:, QKV[n % 2], :], wqkv[w][:, c, m * HD:(m + 1) * HD],
                                     xt[a][:, c, half * BANK:(half + 1) * BANK],
                                     start=k == 0, stop=k == 3 * DC - 1)
                    k += 1
            last.then_inc(qk_mm, 1)

        def v_unit(batch, u):
            if u < 2:
                pe.wait_ge(qk32_ready, batch.n(4, 3 + u))
            else:
                pe.wait_ge(v_done, batch.n(TT, u - 1))
            k = 0
            for a, w in THREE:
                for c in range(DC):
                    last = pe.matmul(ps[:, QKV[u % 2], 0:HD], xt[a][:, c, u * P:(u + 1) * P],
                                     wqkv[w][:, c, 2 * HD:3 * HD], start=k == 0, stop=k == 3 * DC - 1)
                    k += 1
            last.then_inc(v_mm, 1)

        def front(batch):
            for t in range(TT):
                front_tile(batch, t)
            pe.wait_ge(wchunk_split, DC + 2)
            pe.wait_ge(front_lo, batch.n(TT, TT + 1))
            for n in range(4):
                qk_unit(batch, n)
            for u in range(TT):
                v_unit(batch, u)

        def wide(b, i):
            qt, h = i // 4, i % 4
            pe.wait_ge(wide_free, b.n(32, i + 1))
            for k in range(HALF):
                last = pe.matmul(ps[:, WIDE[i % 2] + k, :], qa[:, h // 2, qt * P:(qt + 1) * P],
                                 kz[:, h, k * BANK:(k + 1) * BANK], start=True, stop=True)
            last.then_inc(wide_mm, 1)

        def narrow(b, i):
            qt, h, k = i // 8, 4 + i // 2 % 4, i % 2
            pe.wait_ge(narrow_free, b.n(64, i + 1))
            pe.matmul(ps[:, NARROW[i % 2], :], qa[:, h // 2, qt * P:(qt + 1) * P],
                      kz[:, h, k * BANK:(k + 1) * BANK], start=True, stop=True).then_inc(narrow_mm, 1)

        def scores(b, i):
            unit, kt, pair = i // 16, (i // 2) % TT, i % 2
            g, qh = unit // 2, unit % 2
            pe.wait_ge(exp_done, b.n(PAIRS, i + 1))
            for k in range(2):
                h = 4 * g + 2 * pair + k
                last = pe.matmul(ps[:, ST[i % 2] + k, :], kz[:, h, kt * P:(kt + 1) * P],
                                 qa[:, h // 2, qh * BANK:(qh + 1) * BANK], start=True, stop=True)
            last.then_inc(st_ready, 1)

        def values(b, i):
            unit, kt, pair = i // 16, (i // 2) % TT, i % 2
            g = unit // 2
            if i % 16 == 0:
                pe.wait_ge(o_copied, b.n(4, unit + 1))
            pe.wait_ge(exp_done, b.n(PAIRS, i + 3))
            for k in range(2):
                j = 2 * pair + k
                last = pe.matmul(ps[32 * j:32 * (j + 1), O_BANK, :], v32[:, kt, 4 * g + j, :],
                                 p32[:, i % 4, k, :], start=kt == 0, stop=kt == TT - 1)
            last.then_inc(pv_done, 1)

        def back(b, unit):
            pe.wait_ge(o_copied, b.n(4, unit + 2))
            pe.wait_ge(o_norm, b.n(4, unit + 1))
            for q in range(4):
                last = pe.transpose(ps[:, OT_BANK, q * P:(q + 1) * P], osb[:, unit % 2, q * P:(q + 1) * P],
                                    ident[:])
            last.then_inc(ot_done, 1)

        def output_tile(b, t):
            pe.wait_ge(oolo_done, b.n(TT, t + 1))
            pe.transpose(ps[:, OO_BANK, 0:P], onorm[:, t, :], ident[:]).then_inc(oo_done, 1)
            pe.wait_ge(oolo_done, b.n(TT, t + 2))
            pe.wait_ge(y_done, b.n(TT, t + 1))
            for k in range(2):
                for n, (a, w) in enumerate(THREE):
                    last = pe.matmul(ps[:, Y + k, :], ot[a][:, t % 2, :],
                                     wo[w][:, k * BANK:(k + 1) * BANK], start=n == 0, stop=n == 2)
            last.then_inc(y_mm, 1)

        def tail_tile(b, t):
            pe.wait_ge(tail_norm, b.n(TT, t + 1))
            pe.wait_ge(tail_lo, b.n(TT, t + 1))
            transpose_tile(t % 2, TAIL_TP).then_inc(tail_tp, 1)

        def gate_tile(b, t):
            u = t % GRP
            pe.wait_ge(tail_lo, b.n(TT, t + 2))
            k = 0
            for a, w in THREE:
                for c in range(DC):
                    last = pe.matmul(ps[:, GATE_BANK, t * NE:(t + 1) * NE], ht[a][:, c, u * P:(u + 1) * P],
                                     gw[w][:, c, :], start=k == 0, stop=k == 3 * DC - 1)
                    k += 1
            last.then_inc(gate_mm, 1)

        def iteration(b, ahead):
            b = b.again(pe, "maxima")
            pe.wait_ge(pool_consts, POOL_CONSTS)
            pe.wait_ge(qk_placed, b.n(PLACES * 16, PLACES * 16 + 1))
            pe.wait_ge(y_done, b.n(TT, 1))
            pe.wait_ge(tail_lo, b.n(TT, 1))
            for i in range(32):
                wide(b, i)
            pe.wait_ge(v_done, b.n(TT, TT))
            pe.wait_ge(o_norm, b.n(4, 1))
            pe.wait_ge(wide_free, b.n(32, 32 + 2))
            pe.transpose(ps[:, OT_BANK, 0:P], mrow[:, 0, :], ident[:]).then_inc(mt_done, 1)
            pe.wait_ge(front_lo, b.n(TT, TT + 1))
            pe.wait_ge(oolo_done, b.n(TT, 1))
            pe.wait_ge(gate_done, b.n(1, 1))
            b = b.again(pe, "first")
            for i in range(10):
                narrow(b, i)
            pe.wait_ge(mlo_done, b.n(2, 1))
            pe.wait_ge(m_placed, b.n(128, 64 + 1))
            for i in range(32):
                scores(b, i)
                for k in range(10 + 2 * i, min(12 + 2 * i, 64)):
                    narrow(b, k)
                if i >= 1:
                    values(b, i - 1)
                if i in BACK_AT:
                    back(b, BACK_AT[i])
                if 12 + 2 * i in (64, 65):
                    pe.wait_ge(m_ready, b.n(1, 1))
                    pe.transpose(ps[:, FRONT_TP, 0:P], mrow[:, 1, :], ident[:]).then_inc(mt_done, 1)
            values(b, 31)
            b = b.again(pe, "second")
            pe.wait_ge(mlo_done, b.n(2, 2))
            pe.wait_ge(m_placed, b.n(128, 128 + 1))
            for i in range(32, PAIRS):
                scores(b, i)
                if i > 32:
                    values(b, i - 1)
                if i in BACK_AT:
                    back(b, BACK_AT[i])
                if ahead and i in FRONT_AT:
                    front_tile(b.next(), FRONT_AT[i])
            values(b, PAIRS - 1)
            back(b, 3)
            b = b.again(pe, "tail")
            pe.wait_ge(o_norm, b.n(4, 4 + 1))
            pe.wait_ge(exp_done, b.n(PAIRS, PAIRS + 2))
            if ahead:
                pe.wait_ge(front_lo, b.n(TT, 2 * TT + 1))
            for g in range(NG):
                for t in range(g * GRP, (g + 1) * GRP):
                    output_tile(b, t)
                if ahead:
                    if g == 0:
                        for n in range(4):
                            qk_unit(b.next(), n)
                    else:
                        for u in range(TT):
                            v_unit(b.next(), u)
                for t in range(g * GRP, (g + 1) * GRP + 1):
                    if t < (g + 1) * GRP:
                        tail_tile(b, t)
                    if t > g * GRP:
                        gate_tile(b, t - 1)
            pe.wait_ge(sums_ready, b.n(1, 1))
            pe.matmul(ps[:, OO_BANK, 0:2], ones[:], parts[:], start=True, stop=True).then_inc(sums_mm, 1)

        pe.wait_ge(pool_consts, 3)
        each_batch(pe, front, iteration)

    @block.scalar
    def _(act):
        def high(dst, t, banks, done):
            src = ps[:, banks:banks + 2, :].rearrange("p a (c q) -> p (a c) q", q=P)
            nc.scalar.activation(dst[:, :, t * P:(t + 1) * P], src, ACT.Copy).then_inc(done, 1)

        def front_tile(batch, t):
            act.wait_ge(front_tp, batch.n(TT, t + 3))
            high(xt[0], t, FRONT_TP, front_hi)

        def qk_unit(batch, n):
            act.wait_ge(qk_mm, batch.n(4, n + 1))
            act.wait_ge(qk_split, batch.n(4, n + 1))
            nc.scalar.activation(qk32[:, n % 2, :], ps[:, QKV[n % 2], :], ACT.Identity,
                                 bias=bqk[:, n % 2:n % 2 + 1], scale=1.0 / WS).then_inc(qk32_ready, 1)

        def front(batch):
            for t in range(TT):
                front_tile(batch, t)
            act.wait_ge(const_in, NCONST * 16)
            for n in range(4):
                qk_unit(batch, n)

        def maxima_high(b, g):
            act.wait_ge(mt_done, b.n(2, g + 2))
            act.wait_ge(m_stored, b.n(64, 1))
            bank = (OT_BANK, FRONT_TP)[g]
            nc.scalar.activation(ms[0][:, g, :], ps[:, bank, 0:P], ACT.Copy).then_inc(mhi_done, 1)

        def copy_out(b, unit):
            act.wait_ge(pv_done, b.n(PAIRS, 16 * (unit + 1) + 4))
            act.wait_ge(ot_done, b.n(4, unit + 1))
            nc.scalar.activation(osb[:, unit % 2, :], ps[:, O_BANK, :], ACT.Copy).then_inc(o_copied, 1)

        def probs(b, i):
            act.wait_ge(st_ready, b.n(PAIRS, i + 1))
            act.wait_ge(pv_done, b.n(PAIRS, i + 1))
            nc.scalar.activation(p32[:, i % 4], ps[:, ST[i % 2]:ST[i % 2] + 2, :], ACT.Exp).then_inc(exp_done, 1)
            if i % 16 == 0 and i:
                copy_out(b, i // 16 - 1)

        def iteration(b, ahead):
            b = b.again(act, "first")
            maxima_high(b, 0)
            for i in range(32):
                probs(b, i)
                if 12 + 2 * i in (64, 65):
                    maxima_high(b, 1)
            b = b.again(act, "second")
            for i in range(32, PAIRS):
                probs(b, i)
                if ahead and i in FRONT_AT:
                    front_tile(b.next(), FRONT_AT[i])
            copy_out(b, 3)
            b = b.again(act, "tail")
            for g in range(NG):
                for t in range(g * GRP, (g + 1) * GRP):
                    act.wait_ge(oo_done, b.n(TT, t + 1))
                    nc.scalar.activation(ot[0][:, t % 2, :], ps[:, OO_BANK, 0:P], ACT.Copy).then_inc(oohi_done, 1)
                if ahead and g == 0:
                    for n in range(4):
                        qk_unit(b.next(), n)
                act.wait_ge(ht_stored, b.n(64, 32 * g + 1))
                for t in range(g * GRP, (g + 1) * GRP):
                    act.wait_ge(tail_tp, b.n(TT, t + 3))
                    high(ht[0], t % GRP, TAIL_TP, tail_hi)
                    act.wait_ge(abs_done, b.n(TT, t + 2))
                    nc.scalar.activation(habs[:], xn[:, t % 2, :], ACT.Abs, accum_out=asum[:, t:t + 1]
                                         ).then_inc(abs_done, 1)
            act.wait_ge(lg_ready, b.n(1, 1))
            nc.scalar.activation(sc[:], lg[:], ACT.Exp).then_inc(lg_exp, 1)

        each_batch(act, front, iteration)

    @block.vector
    def _(dve):
        steps = {"batch": Batch(None, 0), "before": 0, "now": 0}

        def link(ins):
            steps["now"] += 1
            ins.then_inc(dve_step, 1)
            value = steps["batch"].n(PER_BATCH, steps["before"] + steps["now"])
            if steps["batch"].reg is None:
                dve.wait_ge(dve_step, value)
            else:
                wait_apart(dve, dve_step, value, passed)

        def split(dst_hi, dst_lo, src):
            link(nc.vector.tensor_scalar(dst_hi, src, WS, None, ALU.mult))
            return nc.vector.scalar_tensor_tensor(out=dst_lo, in0=src, scalar=WS, in1=dst_hi, op0=ALU.mult,
                                                  op1=ALU.subtract)

        def tile_stats(u, src):
            for k in range(2):
                last = nc.vector.bn_stats(stats[:, u, k, :], src[:, k * BANK:(k + 1) * BANK])
            return last

        def group_stats(last, number):
            link(last)
            for u in range(GRP):
                last = nc.vector.bn_aggr(mv[:, u, :], stats[:, u].rearrange("p k s -> p (k s)"))
            last.then_inc(stat_ready, 1)
            dve.wait_ge(rstd_ready, number + 1)

        def normalise(dst, src, u):
            return nc.vector.tensor_scalar(dst, src, mv[:, u, 0:1], rstd[:, u:u + 1], ALU.subtract, ALU.mult)

        def low(dst, t, banks):
            src = ps[:, banks:banks + 2, :].rearrange("p a (c q) -> p (a c) q", q=P)
            return nc.vector.tensor_tensor(dst[1][:, :, t * P:(t + 1) * P], src, dst[0][:, :, t * P:(t + 1) * P],
                                           ALU.subtract)

        def front_group(batch, g, busy):
            for u in range(GRP):
                t = g * GRP + u
                dve.wait_ge(xa_landed[t % GRP], batch.n(NG * 16, (t // GRP + 1) * 16))
                last = tile_stats(u, xa[:, u, :])
            group_stats(last, round_of(batch, True, g))
            if busy is not None and g == 0:
                dve.wait_ge(tail_tp, busy.n(TT, 2))
                dve.wait_ge(abs_done, busy.n(TT, 2))
            for u in range(GRP + 1):
                t = g * GRP + u
                if u < GRP:
                    dve.wait_ge(front_tp, batch.n(TT, t + 1))
                    normalise(xn[:, t % 2, :], xa[:, t % GRP, :], u).then_inc(front_norm, 1)
                if u:
                    dve.wait_ge(front_hi, batch.n(TT, t))
                    low(xt, t - 1, FRONT_TP).then_inc(front_lo, 1)

        def qk_unit(batch, n):
            half, m = n // 2, n % 2
            cols = slice(half * BANK, (half + 1) * BANK)
            if n == 0:
                dve.wait_ge(qk_stored, batch.n(64, 1))
            dve.wait_ge(qk32_ready, batch.n(4, n + 1))
            link(nc.vector.tensor_copy(qks[m][0][:, cols], qk32[:, n % 2, :]))
            nc.vector.tensor_tensor(qks[m][1][:, cols], qk32[:, n % 2, :], qks[m][0][:, cols],
                                    ALU.subtract).then_inc(qk_split, 1)

        def v_unit(batch, t):
            dve.wait_ge(v_mm, batch.n(TT, t + 1))
            nc.vector.scalar_tensor_tensor(
                out=v32[:, t, :, 0:E], in0=ps[:, QKV[t % 2], 0:HD].rearrange("p (h e) -> p h e", h=H),
                scalar=1.0 / WS, in1=bv[:].rearrange("p (h e) -> p h e", h=H), op0=ALU.mult,
                op1=ALU.add).then_inc(v_done, 1)

        def front(batch):
            front_group(batch, 0, None)
            front_group(batch, 1, None)
            dve.wait_ge(const_in, NCONST * 16)
            split(wo[0][:], wo[1][:], y4[:, 0, :]).then_inc(wchunk_split, 1)
            split(gw[0][:], gw[1][:], gstage[:]).then_inc(wchunk_split, 1)
            for c in range(DC):
                dve.wait_ge(wchunk_in, (c + 1) * 16)
                split(wqkv[0][:, c, :], wqkv[1][:, c, :], wstage[:]).then_inc(wchunk_split, 1)
            for n in range(4):
                qk_unit(batch, n)
            dve.wait_ge(pool_consts, POOL_CONSTS)
            for t in range(TT):
                v_unit(batch, t)
            steps["before"], steps["now"] = steps["now"], 0

        def maxima_low(b, g):
            dve.wait_ge(mhi_done, b.n(2, g + 1))
            bank = (OT_BANK, FRONT_TP)[g]
            nc.vector.tensor_tensor(ms[1][:, g, :], ps[:, bank, 0:P], ms[0][:, g, :], ALU.subtract
                                    ).then_inc(mlo_done, 1)

        def narrow(b, i):
            dve.wait_ge(narrow_mm, b.n(64, i + 1))
            qt, h, k = i // 8, i // 2 % 4, i % 2
            return nc.vector.reduce_max(mpart[:, h * TT + qt, k:k + 1], ps[:, NARROW[i % 2], :], AX.X
                                        ).then_inc(narrow_free, 1)

        def head_outputs(b, unit):
            g, qh = unit // 2, unit % 2
            dve.wait_ge(ot_done, b.n(4, unit + 3))
            o4 = ps[:, OT_BANK, :].rearrange("p (q j e) -> p q j e", q=4, j=4)
            link(nc.vector.reciprocal(rinv[:], o4[:, :, :, E:E + 1]))
            for q in range(4):
                last = nc.vector.tensor_tensor(
                    onorm[:, 4 * qh + q, 4 * E * g:4 * E * (g + 1)].rearrange("p (j e) -> p j e", j=4),
                    o4[:, q, :, 0:E], rinv[:, q].to_broadcast([P, 4, E]), ALU.mult)
            last.then_inc(o_norm, 1)

        def output_tile(b, t):
            u = t % GRP
            dve.wait_ge(oohi_done, b.n(TT, t + 1))
            nc.vector.tensor_tensor(ot[1][:, t % 2, :], ps[:, OO_BANK, 0:P], ot[0][:, t % 2, :],
                                    ALU.subtract).then_inc(oolo_done, 1)
            dve.wait_ge(y_mm, b.n(TT, t + 1))
            nc.vector.scalar_tensor_tensor(
                out=y4[:, u, :], in0=ps[:, Y:Y + 2, :].rearrange("p a n -> p (a n)"),
                scalar=1.0 / (WS * float(HD) ** 0.5), in1=bo[:], op0=ALU.mult, op1=ALU.add).then_inc(y_done, 1)

        def iteration(b, ahead):
            steps["batch"], steps["now"] = b, 0
            b = b.again(dve, "maxima")
            dve.wait_ge(mt_done, b.n(2, 1))
            for i in range(32):
                qt, h = i // 4, i % 4
                dve.wait_ge(wide_mm, b.n(32, i + 1))
                nc.vector.reduce_max(mrow[:, 0, h * TT + qt:h * TT + qt + 1],
                                     ps[:, WIDE[i % 2]:WIDE[i % 2] + 2, :].rearrange("p a n -> p (a n)"),
                                     AX.X).then_inc(wide_free, 1)
            maxima_low(b, 0)
            b = b.again(dve, "first")
            steps["batch"] = b
            backs = {10 + 2 * i: unit for i, unit in BACK_AT.items()}
            for i in range(64):
                if i in backs:
                    head_outputs(b, backs[i])
                narrow(b, i)
            dve.wait_ge(narrow_free, b.n(64, 64 + 2))
            nc.vector.tensor_tensor(mrow[:, 1, 0:32], mpart[:, :, 0], mpart[:, :, 1], ALU.max).then_inc(m_ready, 1)
            maxima_low(b, 1)
            b = b.again(dve, "second")
            steps["batch"] = b
            for unit in range(1, 4):
                head_outputs(b, unit)
                if ahead and unit < 3:
                    front_group(b.next(), unit - 1, b)
            b = b.again(dve, "tail")
            steps["batch"] = b
            for g in range(NG):
                group = range(g * GRP, (g + 1) * GRP)
                dve.wait_ge(x1_stored, b.n(NG * 16, g * 16 + 1))
                for t in group:
                    output_tile(b, t)
                    dve.wait_ge(y_done, b.n(TT, t + 2))
                    last = tile_stats(t % GRP, y4[:, t % GRP, :])
                group_stats(last, round_of(b, False, 2 * g, ahead))
                for u in range(GRP):
                    last = normalise(y4[:, u, :], y4[:, u, :], u)
                link(last)
                for t in group:
                    u = t % GRP
                    dve.wait_ge(xres_landed[u], b.n(NG * 16, (g + 1) * 16))
                    nc.vector.tensor_tensor(y4[:, u, :], y4[:, u, :], xres[:, u, :], ALU.add).then_inc(x1_done, 1)
                if ahead and g == 0:
                    qk_unit(b.next(), 0)
                    qk_unit(b.next(), 1)
                dve.wait_ge(x1_done, b.n(TT, (g + 1) * GRP + GRP))
                for u in range(GRP):
                    last = tile_stats(u, y4[:, u, :])
                group_stats(last, round_of(b, False, 2 * g + 1, ahead))
                if ahead:
                    if g == 0:
                        qk_unit(b.next(), 2)
                        qk_unit(b.next(), 3)
                    else:
                        for t in range(TT):
                            v_unit(b.next(), t)
                if g == 0:
                    dve.wait_ge(front_tp, b.n(TT, (2 if ahead else 1) * TT + 2))
                for t in range(g * GRP, (g + 1) * GRP + 1):
                    if t < (g + 1) * GRP:
                        dve.wait_ge(tail_tp, b.n(TT, t + 1))
                        dve.wait_ge(abs_done, b.n(TT, t + 1))
                        normalise(xn[:, t % 2, :], y4[:, t % GRP, :], t % GRP).then_inc(tail_norm, 1)
                    if t > g * GRP:
                        dve.wait_ge(tail_hi, b.n(TT, t))
                        low(ht, (t - 1) % GRP, TAIL_TP).then_inc(tail_lo, 1)
            b = b.again(dve, "gate")
            steps["batch"] = b
            dve.wait_ge(abs_done, b.n(TT, TT + 2))
            nc.vector.reduce_sum(gs[:, 0:1], asum[:, 0:SPLIT_TILE], AX.X)
            link(nc.vector.reduce_sum(gs[:, 1:2], asum[:, SPLIT_TILE:TT], AX.X))
            link(nc.vector.tensor_tensor(gs[:, 2:3], asum[:, SPLIT_TILE:SPLIT_TILE + 1], vision_rows[:], ALU.mult))
            nc.vector.tensor_tensor(parts[:, 0:1], gs[:, 0:1], gs[:, 2:3], ALU.add)
            nc.vector.tensor_tensor(parts[:, 1:2], gs[:, 1:2], gs[:, 2:3], ALU.subtract).then_inc(sums_ready, 1)
            dve.wait_ge(sums_mm, b.n(1, 1))
            link(nc.vector.tensor_scalar(gs[:, 3:4], ps[:, OO_BANK, 0:1], 1.0 / (VISION * D), 1e-8, ALU.mult, ALU.add))
            link(nc.vector.reciprocal(gs[:, 4:5], gs[:, 3:4]))
            link(nc.vector.scalar_tensor_tensor(out=gs[:, 5:6], in0=ps[:, OO_BANK, 1:2], scalar=1.0 / ((NT - VISION) * D),
                                                in1=gs[:, 4:5], op0=ALU.mult, op1=ALU.mult))
            link(nc.vector.scalar_tensor_tensor(out=gbase[:], in0=gw_ratio[:], scalar=gs[:, 5:6], in1=gate_b[:],
                                                op0=ALU.mult, op1=ALU.add))
            dve.wait_ge(gate_mm, b.n(TT, TT))
            link(nc.vector.scalar_tensor_tensor(
                out=lg[:], in0=ps[:, GATE_BANK, 0:TT * NE].rearrange("p (t e) -> p t e", e=NE), scalar=1.0 / WS,
                in1=gbase[:].unsqueeze(1).to_broadcast([P, TT, NE]), op0=ALU.mult, op1=ALU.add))
            g2 = g1[:].unsqueeze(3)
            link(nc.vector.reduce_max(g2[:, 0], lg[:], AX.X))
            nc.vector.tensor_tensor(lg[:], lg[:], g2[:, 0].to_broadcast([P, TT, NE]), ALU.subtract
                                    ).then_inc(lg_ready, 1)
            dve.wait_ge(lg_exp, b.n(1, 1))
            link(nc.vector.reduce_sum(g2[:, 1], sc[:], AX.X))
            link(nc.vector.reciprocal(g2[:, 2], g2[:, 1]))
            link(nc.vector.tensor_tensor(sc[:], sc[:], g2[:, 2].to_broadcast([P, TT, NE]), ALU.mult))
            nc.vector.reduce_max(g2[:, 3], sc[:], AX.X)
            nc.vector.tensor_tensor(g2[:, 4], sc[:, :, 0:1], sc[:, :, 1:2], ALU.min)
            link(nc.vector.tensor_tensor(g2[:, 5], sc[:, :, 0:1], sc[:, :, 1:2], ALU.max))
            link(nc.vector.tensor_tensor(g2[:, 5], g2[:, 5], sc[:, :, 2:3], ALU.min))
            link(nc.vector.tensor_tensor(g2[:, 4], g2[:, 4], g2[:, 5], ALU.max))
            link(nc.vector.scalar_tensor_tensor(out=g2[:, 6], in0=g2[:, 3], scalar=1e-8, in1=g2[:, 4],
                                                op0=ALU.add, op1=ALU.add))
            link(nc.vector.reciprocal(g2[:, 7], g2[:, 6]))
            for k in range(2):
                nc.vector.tensor_tensor(keep["tv"][:, bass.ds(b.n(2 * TT, k * TT), TT)], g1[:, 3 + k, :],
                                        g1[:, 7, :], ALU.mult)
            a, c, d = (sc[0:1, 0, k:k + 1] for k in range(NE))

            def flag(k, x, y, op):
                return nc.vector.tensor_tensor(jt[:, k:k + 1], x, y, op)

            flag(0, a, c, ALU.is_ge)
            flag(1, a, d, ALU.is_ge)
            flag(2, c, d, ALU.is_ge)
            flag(3, c, a, ALU.is_le)
            flag(4, d, a, ALU.is_le)
            link(flag(5, d, c, ALU.is_le))
            flag(6, jt[:, 0:1], jt[:, 1:2], ALU.mult)
            link(flag(7, jt[:, 4:5], jt[:, 5:6], ALU.mult))
            nc.vector.tensor_scalar(jt[:, 8:9], jt[:, 6:7], -1.0, 1.0, ALU.mult, ALU.add)
            nc.vector.tensor_scalar(jt[:, 9:10], jt[:, 2:3], -1.0, 2.0, ALU.mult, ALU.add)
            link(nc.vector.tensor_scalar(jt[:, 10:11], jt[:, 3:4], -1.0, 2.0, ALU.mult, ALU.add))
            flag(11, jt[:, 8:9], jt[:, 9:10], ALU.mult)
            link(flag(12, jt[:, 7:8], jt[:, 10:11], ALU.mult))
            link(flag(13, jt[:, 12:13], jt[:, 3:4], ALU.add))
            link(flag(14, jt[:, 11:12], jt[:, 13:14], ALU.add))
            nc.vector.tensor_copy(keep["jobs"][:, bass.ds(b.n(2), 1)], jt[:, 11:12])
            nc.vector.tensor_scalar(keep["jobs"][:, bass.ds(b.n(2, 1), 1)], jt[:, 14:15], -1.0, 3.0, ALU.mult,
                                    ALU.add).then_inc(gate_done, 1)
            if ahead:
                assert steps["now"] == PER_BATCH, steps["now"]

        each_batch(dve, front, iteration)


PER_BATCH = 38


def expert_phase(nc, io, scr, keep, out, ctx):

    def sb(name, shape, dt=F32):
        return ctx.enter_context(nc.sbuf_tensor(name, shape, dt))

    def sem(name):
        return ctx.enter_context(nc.semaphore(name))

    ps1 = ctx.enter_context(nc.psum_tensor("ps1", [P, 2, NT], F32))
    ps2 = ctx.enter_context(nc.psum_tensor("ps2", [P, 2, D], F32))
    JOBS = 2 * NB

    stage = keep["ring"]
    w1 = keep["wide16"]
    w2 = [sb(f"w2{i}", [P, DC, D], F16) for i in range(2)]
    ht = [keep["kz"], sb("ht_low", [P, DC, NT], F16)]
    hid = [sb(f"hid{i}", [P, DC, NT], F16) for i in range(2)]
    act32 = sb("act32", [P, 2, NT])
    b2bc = sb("b2bc", [P, D])
    etmp = sb("etmp", [P, 2, D])
    moe = sb("moe", [P, TT, D])
    x1b = sb("x1b", [P, D])
    stats = sb("stats2", [P, 2, 2, 6])
    mv = sb("mv2", [P, 2, 2])
    std = sb("std2", [P, 2])
    rstd = sb("rstd2", [P, 2])
    epsc = sb("epsc", [P, 1])

    stage_landed = [sem(f"stage_landed{i}") for i in range(STAGE)]
    chunk_split = sem("chunk_split")
    pool_step2 = sem("pool_step2")
    ht_landed = [sem(f"ht_landed{i}") for i in range(2)]
    b2_landed = sem("b2_landed")
    mm1_done = sem("mm1_done")
    mm2_done = sem("mm2_done")
    act_done = sem("act_done")
    hidden_hi = sem("hidden_hi")
    hidden_split = sem("hidden_split")
    evac_done = sem("evac_done")
    etmp_done = sem("etmp_done")
    eps_ready = sem("eps_ready")
    var_ready = sem("var_ready")
    std_ready = sem("std_ready")
    dve_step2 = sem("dve_step2")
    x1_landed = sem("x1_landed")
    norm_done = sem("norm_done")
    y_ready = sem("y_ready")
    y_stored = [sem(f"y_stored{i}") for i in range(2)]
    passed2 = sem("passed2")

    w_dram = (io["w1"].rearrange("e (c p) n -> e c p n", p=P), io["w2"].rearrange("e (c p) n -> e c p n", p=P))
    out_v = out.rearrange("b (t p) d -> (b t) p d", p=P)
    x1_v = scr["x1"].rearrange("b (t p) d -> (b t) p d", p=P)
    block = ctx.enter_context(nc.Block())

    @block.sync
    def _(sp):
        def load_weights(b, s, which, before):
            e = sp.value_load(keep["jobs"][:, bass.ds(b.n(2, s), 1)], min_val=0, max_val=NE - 1)
            for c in range(DC):
                sp.wait_ge(chunk_split, b.n(4 * DC, before + c + 1))
                sp.dma_start(stage[:, c % STAGE, :], w_dram[which][bass.ds(e, 1), c].rearrange("o p n -> (o p) n")
                             ).then_inc(stage_landed[c % STAGE], 16)
                if which == 1 and c == STAGE - 1:
                    sp.wait_ge(evac_done, b.n(2 * TT, s * TT + 2))
                    sp.dma_start(b2bc[:], io["b2"][bass.ds(e, 1)].to_broadcast([P, D])).then_inc(b2_landed, 16)

        def load_h(b, i):
            sp.dma_start(ht[i][:], scr["ht"][i][bass.ds(b.n(1), 1)].rearrange("o p c t -> (o p) c t")
                         ).then_inc(ht_landed[i], 16)

        def iteration(b, ahead):
            load_weights(b, 0, 1, 0)
            load_weights(b, 1, 0, DC)
            load_weights(b, 1, 1, 2 * DC)
            if ahead:
                b = b.again(sp, "next")
                sp.wait_ge(mm1_done, b.n(2 * TT, 2 * TT + 1))
                for i in range(2):
                    load_h(b.next(), i)
                load_weights(b, 2, 0, 3 * DC)

        load_h(Batch(None, 0), 1)
        with sp.Fori(0, NB - 1) as b:
            iteration(Batch(b), True)
        iteration(Batch(None, NB - 1), False)

    @block.gpsimd
    def _(pool):
        add_credits(pool, [(chunk_split, STAGE), (act_done, 2), (hidden_split, 2), (evac_done, 2),
                           (mm1_done, 1), (mm2_done, 1), (y_ready, 1), (y_stored[0], 1), (y_stored[1], 1),
                           (ht_landed[0], 16)])

        def layer(job, which):
            pool.wait_ge((mm1_done, mm2_done)[which], job.n(TT, (1 - which) * TT + 1))
            for c in range(DC):
                k = (1 - which) * DC + c
                wait_apart(pool, stage_landed[c % STAGE], job.n(2 * DC // STAGE * 16, (k // STAGE + 1) * 16), passed2)
                split_weights(nc, pool, (w1, w2)[which], c, stage[:, c % STAGE, :], pool_step2,
                              job.n(4 * DC, 2 * k), lambda s, v: wait_apart(pool, s, v, passed2)
                              ).then_inc(chunk_split, 1)

        with pool.Fori(0, JOBS - 1) as job:
            layer(Batch(job), 1)
            layer(Batch(job), 0)
        layer(Batch(None, JOBS - 1), 1)

    @block.tensor
    def _(pe):
        with pe.Fori(0, NB) as b:
            for s in range(2):
                if s == 0:
                    for i in range(2):
                        wait_apart(pe, ht_landed[i], (b + 1) * 16, passed2)
                wait_apart(pe, chunk_split, b * (4 * DC) + (s * 2 * DC + STAGE), passed2)
                with pe.Fori(0, TT // 2) as pair:
                    f0 = pair * 2
                    for u in range(2):
                        pe.wait_ge(act_done, b * (2 * TT) + f0 + (s * TT + u + 1))
                        for half in range(HALF):
                            k = 0
                            for a, w in ((0, 0), (1, 0), (0, 1)):
                                for c in range(DC):
                                    last = pe.matmul(ps1[:, u, half * BANK:(half + 1) * BANK],
                                                     w1[w][:, c, bass.ds(f0 * P + u * P, P)],
                                                     ht[a][:, c, half * BANK:(half + 1) * BANK],
                                                     start=k == 0, stop=k == 3 * DC - 1)
                                    k += 1
                        last.then_inc(mm1_done, 1)
                pe.wait_ge(chunk_split, b * (4 * DC) + (s * 2 * DC + DC + STAGE))
                wait_apart(pe, hidden_split, b * (2 * TT) + ((s + 1) * TT + 2), passed2)
                with pe.Fori(0, TT // 2) as pair:
                    t0 = pair * 2
                    for u in range(2):
                        pe.wait_ge(evac_done, b * (2 * TT) + t0 + (s * TT + u + 1))
                        for half in range(HALF):
                            k = 0
                            for a, w in ((0, 0), (1, 0), (0, 1)):
                                for c in range(DC):
                                    last = pe.matmul(ps2[:, u, half * BANK:(half + 1) * BANK],
                                                     hid[a][:, c, bass.ds(t0 * P + u * P, P)],
                                                     w2[w][:, c, half * BANK:(half + 1) * BANK],
                                                     start=k == 0, stop=k == 3 * DC - 1)
                                    k += 1
                        last.then_inc(mm2_done, 1)

    @block.scalar
    def _(act):
        def hidden_tiles(b, s, e, func):
            with act.Fori(0, TT // 2) as pair:
                f0 = pair * 2
                for u in range(2):
                    act.wait_ge(mm1_done, b * (2 * TT) + f0 + (s * TT + u + 1) + 1)
                    act.wait_ge(hidden_split, b * (2 * TT) + f0 + (s * TT + u + 1))
                    nc.scalar.activation(act32[:, u, :], ps1[:, u, :], func,
                                         bias=keep["b1"][:, bass.ds(f0 + (e * DC + u), 1)], scale=1.0 / WS
                                         ).then_inc(act_done, 1)

        act.wait_ge(eps_ready, 1)
        with act.Fori(0, NB) as b:
            for s in range(2):
                j = act.value_load(keep["jobs"][:, bass.ds(b * 2 + s, 1)], min_val=0, max_val=NE - 1)
                for e, func in enumerate((ACT.Tanh, ACT.Gelu, ACT.Silu)):
                    with act.If(j == e):
                        hidden_tiles(b, s, e, func)
            with act.Fori(0, TT // 2) as pair:
                for u in range(2):
                    t = b * TT + pair * 2 + u
                    act.wait_ge(y_ready, t + 1)
                    act.dma_start(x1b[:], x1_v[bass.ds(t, 1)].rearrange("o p d -> (o p) d")).then_inc(x1_landed, 16)
                    act.wait_ge(var_ready, t + 1)
                    nc.scalar.activation(std[:, u:u + 1], mv[:, u, 1:2], ACT.Sqrt, bias=epsc[:]
                                         ).then_inc(std_ready, 1)
                    act.wait_ge(y_ready, t + 2)
                    act.dma_start(out_v[bass.ds(t, 1)].rearrange("o p d -> (o p) d"), etmp[:, u, :]
                                  ).then_inc(y_stored[u], 16)
        for u in range(2):
            act.wait_ge(y_stored[u], NB * TT // 2 * 16 + 1)

    @block.vector
    def _(dve):
        nc.vector.memset(epsc[:], EPS).then_inc(eps_ready, 1)
        with dve.Fori(0, NB) as b:
            for s in range(2):
                wait_apart(dve, mm2_done, b * (2 * TT) + s * TT + 1, passed2)
                with dve.Fori(0, TT // 2) as pair:
                    f0 = pair * 2
                    for u in range(2):
                        n = b * (2 * TT) + f0 + (s * TT + u)
                        dve.wait_ge(act_done, n + 3)
                        nc.vector.tensor_copy(hid[0][:, bass.ds(f0 + u, 1), :].rearrange("p o n -> p (o n)"),
                                              act32[:, u, :]).then_inc(hidden_hi, 1)
                        dve.wait_ge(hidden_hi, n + 1)
                        nc.vector.tensor_tensor(hid[1][:, bass.ds(f0 + u, 1), :].rearrange("p o n -> p (o n)"),
                                                act32[:, u, :],
                                                hid[0][:, bass.ds(f0 + u, 1), :].rearrange("p o n -> p (o n)"),
                                                ALU.subtract).then_inc(hidden_split, 1)
                wait_apart(dve, b2_landed, b * 32 + (s + 1) * 16, passed2)
                if s == 0:
                    for u in range(2):
                        wait_apart(dve, y_stored[u], b * (TT // 2 * 16) + 1, passed2)
                with dve.Fori(0, TT // 2) as pair:
                    t0 = pair * 2
                    for u in range(2):
                        n = b * (2 * TT) + t0 + (s * TT + u)
                        m = moe[:, bass.ds(t0 + u, 1), :].rearrange("p o n -> p (o n)")
                        tv = keep["tv"][:, bass.ds(b * (2 * TT) + t0 + (s * TT + u), 1)]
                        if s == 1:
                            wait_apart(dve, y_stored[u], b * (TT // 2 * 16) + pair * 16 + 1, passed2)
                        dve.wait_ge(mm2_done, n + 2)
                        nc.vector.scalar_tensor_tensor(out=etmp[:, u, :], in0=ps2[:, u, :], scalar=1.0 / WS,
                                                       in1=b2bc[:], op0=ALU.mult, op1=ALU.add
                                                       ).then_inc(evac_done, 1)
                        dve.wait_ge(evac_done, n + 3)
                        if s == 0:
                            nc.vector.tensor_scalar(m, etmp[:, u, :], tv, None, ALU.mult).then_inc(etmp_done, 1)
                            continue
                        nc.vector.scalar_tensor_tensor(out=etmp[:, u, :], in0=etmp[:, u, :], scalar=tv, in1=m,
                                                       op0=ALU.mult, op1=ALU.add).then_inc(etmp_done, 1)
                        t = b * TT + t0 + u
                        wait_apart(dve, etmp_done, n + 1, passed2)
                        for k in range(2):
                            last = nc.vector.bn_stats(stats[:, u, k, :], etmp[:, u, k * BANK:(k + 1) * BANK])
                        last.then_inc(dve_step2, 1)
                        wait_apart(dve, dve_step2, t * 2 + 1, passed2)
                        nc.vector.bn_aggr(mv[:, u, :], stats[:, u].rearrange("p k s -> p (k s)")).then_inc(var_ready, 1)
                        dve.wait_ge(std_ready, t + 1)
                        nc.vector.reciprocal(rstd[:, u:u + 1], std[:, u:u + 1]).then_inc(dve_step2, 1)
                        dve.wait_ge(dve_step2, t * 2 + 2)
                        nc.vector.tensor_scalar(etmp[:, u, :], etmp[:, u, :], mv[:, u, 0:1], rstd[:, u:u + 1],
                                                ALU.subtract, ALU.mult).then_inc(norm_done, 1)
                        wait_apart(dve, norm_done, t + 1, passed2)
                        dve.wait_ge(x1_landed, (t + 1) * 16)
                        nc.vector.tensor_tensor(etmp[:, u, :], etmp[:, u, :], x1b[:], ALU.add).then_inc(y_ready, 1)


def sandwich_block(nc, io, out):
    with ExitStack() as ctx:
        keep = {
            "tv": ctx.enter_context(nc.sbuf_tensor("tv", [P, NB * 2 * TT], F32)),
            "jobs": ctx.enter_context(nc.sbuf_tensor("jobs", [1, NB * 2], I32)),
            "b1": ctx.enter_context(nc.sbuf_tensor("b1", [P, NE * DC], F32)),
            "ring": ctx.enter_context(nc.sbuf_tensor("ring", [P, STAGE, D], F32)),
            "wide16": [ctx.enter_context(nc.sbuf_tensor(f"wide16_{i}", [P, DC, NT], F16)) for i in range(2)],
            "kz": ctx.enter_context(nc.sbuf_tensor("kz", [P, H, NT], F16)),
        }
        scr = {
            "qk": nc.dram_tensor("scr_qk", (2, 2, HD, NT), F16).ap(),
            "m": nc.dram_tensor("scr_m", (2, 2, H * TT // 2, P), F16).ap(),
            "x1": nc.dram_tensor("scr_x1", (NB, NT, D), F32).ap(),
            "ht": [nc.dram_tensor(f"scr_ht{i}", (NB, P, DC, NT), F16).ap() for i in range(2)],
        }
        with ExitStack() as phase:
            attention_phase(nc, io, scr, keep, phase)
        with ExitStack() as phase:
            expert_phase(nc, io, scr, keep, out, phase)


def kernel(**inputs):
    import numpy as np
    import concourse.bacc as bacc
    from concourse import mybir as mb
    from concourse.bass_utils import run_bass_kernel_spmd

    a = {k[3:]: np.asarray(v) for k, v in inputs.items()}
    wqk = a["attn_Wqk_w"].reshape(HD, 2, D).transpose(1, 0, 2).reshape(2 * HD, D)
    arrays = {
        "x": a["attn_x"],
        "wqkv_t": np.concatenate([wqk, a["attn_Wv_w"]], 0).T,
        "bqk": a["attn_Wqk_b"].reshape(HD, 2),
        "bv": a["attn_Wv_b"],
        "wo_t": a["attn_Wo_w"].T,
        "bo": a["attn_Wo_b"],
        "gate_w": a["ffn_gate_w"][:D],
        "gw_ratio": a["ffn_gate_w"][D],
        "gate_b": a["ffn_gate_b"],
        "w1": a["ffn_w1"],
        "b1": a["ffn_b1"].reshape(NE, DC, P).transpose(2, 0, 1).reshape(P, NE * DC),
        "w2": a["ffn_w2"],
        "b2": a["ffn_b2"],
    }
    arrays = {k: np.ascontiguousarray(v) for k, v in arrays.items()}
    nc = bacc.Bacc("TRN2", target_bir_lowering=False, num_devices=1)
    io = {k: nc.dram_tensor(f"in_{k}", v.shape, mb.dt.from_np(v.dtype), kind="ExternalInput").ap()
          for k, v in arrays.items()}
    out = nc.dram_tensor("out", (NB, NT, D), mb.dt.float32, kind="ExternalOutput").ap()
    sandwich_block(nc, io, out)
    r = run_bass_kernel_spmd(nc, [{f"in_{k}": v for k, v in arrays.items()}], core_ids=[0])
    return r.results[0]["out"]
```

```python
from contextlib import ExitStack

import concourse.bass as bass
from concourse import mybir

ALU = mybir.AluOpType
ACT = mybir.ActivationFunctionType
AX = mybir.AxisListType
F32 = mybir.dt.float32
F16 = mybir.dt.float16
I32 = mybir.dt.int32

P = 128
NB, NT, D = 4, 1024, 1024
TT = NT // P
DC = D // P
H, E = 8, 16
HD = H * E
HP = H // 2
HR = P // 2
NE = 3
BANK = 512
HALF = NT // BANK
GRP = 4
NG = TT // GRP
VISION = int(NT * 0.3)
SPLIT_TILE, SPLIT_ROW = VISION // P, VISION % P
EPS = 1e-5
WS = 64.0
STAGE = 4


def add_credits(eng, pairs):
    for sem, n in pairs:
        eng.sem_inc(sem, n)


def wait_apart(eng, sem, value, passed):
    eng.wait_ge(sem, value)
    eng.sem_inc(passed, 1)


class Batch:

    def __init__(self, reg, off=0):
        self.reg, self.off = reg, off

    def next(self):
        return Batch(self.reg, self.off + 1)

    def n(self, per_batch, i=0):
        fixed = self.off * per_batch + i
        return fixed if self.reg is None else self.reg * per_batch + fixed

    def again(self, eng, stage):
        if self.reg is None:
            return self
        with eng.register(f"batch_{stage}") as reg:
            eng.reg_mov(reg, self.reg)
            return Batch(eng.snap(reg, min_val=0, max_val=NB - 2), self.off)


def split_weights(nc, pool, w, c, src, step, steps_before, wait):
    nc.gpsimd.tensor_scalar(w[0][:, c, :], src, WS, 1.0, ALU.mult, ALU.mult).then_inc(step, 1)
    wait(step, steps_before + 1)
    nc.gpsimd.tensor_scalar(src, src, WS, 1.0, ALU.mult, ALU.mult).then_inc(step, 1)
    pool.wait_ge(step, steps_before + 2)
    return nc.gpsimd.tensor_tensor(w[1][:, c, :], src, w[0][:, c, :], ALU.subtract)


def attention_phase(nc, io, scr, keep, ctx):

    def sb(name, shape, dt=F32):
        return ctx.enter_context(nc.sbuf_tensor(name, shape, dt))

    def sem(name):
        return ctx.enter_context(nc.semaphore(name))

    ps = ctx.enter_context(nc.psum_tensor("ps", [P, 8, BANK], F32))
    WIDE = (0, 4)
    NARROW = (6, 7)
    ST = (0, 2)
    O_BANK, OT_BANK = 4, 5
    FRONT_TP = 6
    Y, TAIL_TP = 0, 2
    QKV = (4, 5)
    OO_BANK, GATE_BANK = 6, 7

    ident = sb("ident", [P, P])
    ones = sb("ones", [P, P])
    vision_rows = sb("vision_rows", [P, 1])
    half_neg = sb("half_neg", [P, 1])
    eps1 = sb("eps1", [P, 1])
    gstage = sb("gstage", [P, DC, NE])
    wqkv = [sb(f"wqkv{i}", [P, DC, 3 * HD], F16) for i in range(2)]
    wo = [sb(f"wo{i}", [P, D], F16) for i in range(2)]
    gw = [sb(f"gw{i}", [P, DC, NE], F16) for i in range(2)]
    bqk = sb("bqk", [P, 2])
    bv = sb("bv", [P, HD])
    bo = sb("bo", [P, D])
    gw_ratio = sb("gw_ratio", [P, NE])
    gate_b = sb("gate_b", [P, NE])
    xa = keep["ring"]
    xres = sb("xres", [P, GRP, D])
    xn = sb("xn", [P, 2, D])
    xt = keep["wide16"]
    ht = [sb(f"hta{i}", [P, DC, GRP * P], F16) for i in range(2)]
    qk32 = sb("qk32", [P, 2, BANK])
    qks = [[keep["qks"][:, 2 * m + i, :] for i in range(2)] for m in range(2)]
    qa = keep["qa"]
    kz = keep["kz"]
    v32 = sb("v32", [P, TT, H, 32])
    mrow = sb("mrow", [P, 2, P])
    mpart = sb("mpart", [P, 32, 2])
    ms = [sb(f"ms{i}", [P, 2, P], F16) for i in range(2)]
    p32 = sb("p32", [P, 4, 2, BANK])
    osb = sb("osb", [P, 2, BANK])
    rinv = sb("rinv", [P, 4, 4, 1])
    onorm = sb("onorm", [P, TT, HD])
    ot = [sb(f"ot{i}", [P, 2, P], F16) for i in range(2)]
    y4 = sb("y4", [P, GRP, D])
    KINDS = ("x", "y", "x1")
    stats = {kind: sb(f"stats_{kind}", [P, TT, 2, 6]) for kind in KINDS}
    mv = {kind: sb(f"mv_{kind}", [P, TT, 2]) for kind in KINDS}
    vare = {kind: sb(f"vare_{kind}", [P, TT]) for kind in KINDS}
    rstd = {kind: sb(f"rstd_{kind}", [P, TT]) for kind in KINDS}
    shift = {kind: sb(f"shift_{kind}", [P, TT]) for kind in KINDS[1:]}
    habs = sb("habs", [P, D])
    asum = sb("asum", [P, TT])
    parts = sb("parts", [P, 2])
    gs = sb("gs", [P, 8])
    gbase = sb("gbase", [P, NE])
    lg = sb("lg", [P, TT, NE])
    sc = sb("sc", [P, TT, NE])
    g1 = sb("g1", [P, 8, TT])
    jt = sb("jt", [1, 16])

    const_in = sem("const_in")
    wqkv_in = sem("wqkv_in")
    w_split = sem("w_split")
    pool_consts = sem("pool_consts")
    xa_landed = [sem(f"xa_landed{k}") for k in range(GRP)]
    xres_landed = [sem(f"xres_landed{k}") for k in range(GRP)]
    dve_step = sem("dve_step")
    pool_step = sem("pool_step")
    stat_ready = {kind: sem(f"stat_ready_{kind}") for kind in KINDS}
    vare_ready = {kind: sem(f"vare_ready_{kind}") for kind in KINDS}
    rstd_ready = {kind: sem(f"rstd_ready_{kind}") for kind in KINDS}
    shift_ready = {kind: sem(f"shift_ready_{kind}") for kind in KINDS[1:]}
    front_norm = sem("front_norm")
    front_tp = sem("front_tp")
    front_hi = sem("front_hi")
    front_lo = sem("front_lo")
    v_mm = sem("v_mm")
    v_done = sem("v_done")
    qk_mm = sem("qk_mm")
    qk32_ready = sem("qk32_ready")
    qk_split = sem("qk_split")
    qk_stored = sem("qk_stored")
    qk_placed = sem("qk_placed")
    wide_mm = sem("wide_mm")
    wide_free = sem("wide_free")
    narrow_mm = sem("narrow_mm")
    narrow_free = sem("narrow_free")
    m_ready = sem("m_ready")
    mt_done = sem("mt_done")
    mhi_done = sem("mhi_done")
    mlo_done = sem("mlo_done")
    m_stored = sem("m_stored")
    m_placed = sem("m_placed")
    st_ready = sem("st_ready")
    exp_done = sem("exp_done")
    pv_done = sem("pv_done")
    o_copied = sem("o_copied")
    ot_done = sem("ot_done")
    o_norm = sem("o_norm")
    oo_done = sem("oo_done")
    oohi_done = sem("oohi_done")
    oolo_done = sem("oolo_done")
    y_mm = sem("y_mm")
    y_done = sem("y_done")
    y_norm = sem("y_norm")
    x1_done = sem("x1_done")
    x1_stored = [sem(f"x1_stored{k}") for k in range(GRP)]
    tail_norm = sem("tail_norm")
    tail_tp = sem("tail_tp")
    tail_hi = sem("tail_hi")
    tail_lo = sem("tail_lo")
    ht_stored = [sem(f"ht_stored{k}") for k in range(2)]
    abs_done = sem("abs_done")
    gate_mm = sem("gate_mm")
    sums_ready = sem("sums_ready")
    sums_mm = sem("sums_mm")
    lg_ready = sem("lg_ready")
    lg_exp = sem("lg_exp")
    gate_done = sem("gate_done")
    passed = sem("passed")
    ring_landed = [sem(f"ring_landed{k}") for k in range(STAGE)]
    split_step = sem("split_step")
    ring_split = sem("ring_split")
    h0_landed = sem("h0_landed")
    credits = [(front_norm, GRP), (front_tp, 2), (front_lo, 1), (qk_split, 2), (qk_stored, 1), (qk_placed, 1),
               (wide_free, 2), (narrow_free, 2), (mt_done, 1), (m_stored, 1), (m_placed, 1), (exp_done, 2),
               (pv_done, 4), (o_copied, 1), (ot_done, 2), (o_norm, 1), (oolo_done, 1), (y_done, 1),
               (x1_done, GRP), (tail_norm, GRP), (tail_tp, 2), (tail_lo, 1), (abs_done, 2), (gate_done, 1)]
    credits += [(stored, 1) for stored in x1_stored + ht_stored]

    x_v = io["x"].rearrange("b (t p) d -> b p t d", p=P)
    x1_v = scr["x1"].rearrange("b (t p) d -> b p t d", p=P)
    wqkv32 = y4[:].rearrange("p g d -> p (g d)")[:, 0:DC * 3 * HD].rearrange("p (c n) -> p c n", c=DC)
    wo32 = y4[:, GRP - 1, :]
    NCONST = 8
    POOL_CONSTS = 8 + H
    PLACES = 14
    PAIRS = 64
    NARROW_FIRST = 12
    NARROW_LAST_AT = (64 - NARROW_FIRST) // 2 - 1

    FRONT_AT = {34 + 4 * t: t for t in range(TT)}
    BACK_AT = {20: 0, 36: 1, 52: 2}
    STEPS = TT + 7
    QK_AT = {0: ((0, 0), (0, 1)), 1: ((1, 0),), 2: ((1, 1),), 3: ((2, 0),), 4: ((2, 1),), 5: ((3, 0),), 6: ((3, 1),)}
    V_AT = {7: (0, 1), 8: (2, 3), 9: (4, 5), 10: (6, 7)}
    WIDE_AT = {13: (0, 1), 14: (2, 3)}
    WIDE_EARLY = sum(len(units) for units in WIDE_AT.values())
    SUMS_AT = WIDE_EARLY + 4

    def one(ap, batch):
        return ap[bass.ds(batch.n(1), 1)].rearrange("o p t d -> (o p) t d")

    block = ctx.enter_context(nc.Block())

    def each_batch(eng, front, iteration):
        front(Batch(None, 0))
        with eng.Fori(0, NB - 1) as b:
            iteration(Batch(b), True)
        iteration(Batch(None, NB - 1), False)

    @block.sync
    def _(sp):
        def load_front(batch, tiles):
            for t in tiles:
                sp.wait_ge(front_norm, batch.n(TT, t + 1))
                sp.dma_start(xa[:, t % GRP, :], one(x_v, batch)[:, t, :]).then_inc(xa_landed[t % GRP], 16)

        def load_residual(batch, tiles):
            for t in tiles:
                wait_apart(sp, tail_norm, batch.n(TT, t + 1), passed)
                wait_apart(sp, x1_stored[t % GRP], batch.n(NG * 16, t // GRP * 16 + 1), passed)
                sp.dma_start(xres[:, t % GRP, :], one(x_v, batch)[:, t, :]).then_inc(xres_landed[t % GRP], 16)

        def store_qk(batch):
            sp.wait_ge(qk_placed, batch.n(PLACES * 16, 1))
            sp.wait_ge(qk_split, batch.n(4, 4 + 2))
            for m in range(2):
                for i in range(2):
                    sp.dma_start(scr["qk"][m, i], qks[m][i]).then_inc(qk_stored, 16)

        def place_qk(batch):
            wait_apart(sp, qk_stored, batch.n(64, 64 + 1), passed)
            if batch.reg is not None:
                sp.wait_ge(pv_done, batch.n(PAIRS, 4))
            else:
                sp.wait_ge(pool_consts, POOL_CONSTS)
            for j in range(2):
                for slot in range(3):
                    r = j * HR + slot * E
                    qpart, kpart = slot % 2, slot // 2
                    src = scr["qk"].rearrange("m i (hp j e) t -> m i j e hp t", hp=HP, j=2)
                    sp.dma_start(qa[r:r + E], src[0, qpart, j]).then_inc(qk_placed, 16)
                    kdst = kz[r:r + E].rearrange("e (hp j) t -> e j hp t", j=2)[:, j]
                    sp.dma_start(kdst, src[1, kpart, j]).then_inc(qk_placed, 16)
                r = j * HR + 3 * E
                sp.dma_start(qa[r:r + 2], kz[3 * E + 4:3 * E + 6, 0:HP, :]).then_inc(qk_placed, 16)

        def place_maxima(batch, g):
            wait_apart(sp, m_placed, batch.n(128, 1), passed)
            sp.wait_ge(mlo_done, batch.n(2, g + 1))
            for i in range(2):
                sp.dma_start(scr["m"][g, i], ms[i][0:32, g, :]).then_inc(m_stored, 16)
            sp.wait_ge(m_stored, batch.n(64, 32 * (g + 1) + 1))
            for i in range(2):
                for j in range(2):
                    r = j * HR + 3 * E + i
                    src = scr["m"].rearrange("g i (hp j q) n -> g i j hp (q n)", hp=2, j=2)[g, i, j]
                    sp.dma_start(qa[r:r + 1, 2 * g:2 * g + 2], src.unsqueeze(0)).then_inc(m_placed, 16)

        def store_x1(batch, t):
            sp.wait_ge(x1_done, batch.n(TT, t + 1 + GRP))
            sp.dma_start(one(x1_v, batch)[:, t, :], xres[:, t % GRP, :]).then_inc(x1_stored[t % GRP], 16)

        def store_ht(batch, pair):
            wait_apart(sp, tail_lo, batch.n(TT, 2 * pair + 2 + 1), passed)
            slot = pair % 2
            for i in range(2):
                sp.dma_start(one(scr["ht"][i], batch)[:, :, 2 * pair * P:2 * (pair + 1) * P],
                             ht[i][:, :, 2 * slot * P:2 * (slot + 1) * P]).then_inc(ht_stored[slot], 16)

        def load_expert(chunks):
            if chunks[0] == 0:
                sp.wait_ge(gate_done, 1 + 1)
                sp.wait_ge(front_norm, NB * TT + GRP)
            e = sp.value_load(keep["jobs"][:, 0:1], min_val=0, max_val=NE - 1)
            for c in chunks:
                if c >= STAGE:
                    sp.wait_ge(ring_split, c - STAGE + 1)
                sp.dma_start(xa[:, c % STAGE, :], io["w1"].rearrange("e (c p) n -> e c p n", p=P)[bass.ds(e, 1), c]
                             .rearrange("o p n -> (o p) n")).then_inc(ring_landed[c % STAGE], 16)

        def front(batch):
            load_front(batch, range(GRP))
            sp.dma_start(wqkv32, io["wqkv_t"].rearrange("(c p) n -> p c n", p=P)).then_inc(wqkv_in, 16)
            load_front(batch, range(GRP, TT))
            sp.dma_start(bqk[:], io["bqk"]).then_inc(const_in, 16)
            sp.dma_start(bv[:], io["bv"].partition_broadcast(P)).then_inc(const_in, 16)
            sp.dma_start(bo[:], io["bo"].partition_broadcast(P)).then_inc(const_in, 16)
            sp.dma_start(gw_ratio[:], io["gw_ratio"].partition_broadcast(P)).then_inc(const_in, 16)
            sp.dma_start(gate_b[:], io["gate_b"].partition_broadcast(P)).then_inc(const_in, 16)
            sp.dma_start(gstage[:], io["gate_w"].rearrange("(c p) e -> p c e", p=P)).then_inc(const_in, 16)
            sp.dma_start(wo32, io["wo_t"]).then_inc(const_in, 16)
            sp.dma_start(keep["b1"][:], io["b1"]).then_inc(const_in, 16)
            store_qk(batch)
            place_qk(batch)

        def iteration(b, ahead):
            load_residual(b, range(GRP))
            if ahead:
                load_front(b.next(), range(GRP))
            else:
                load_expert(range(STAGE))
            for g in range(2):
                place_maxima(b, g)
                if g == 0 and not ahead:
                    load_expert(range(STAGE, DC))
            if ahead:
                load_front(b.next(), range(GRP, TT))
            if not ahead:
                sp.wait_ge(ht_stored[0], 64 + 1)
                sp.wait_ge(ht_stored[1], 64 + 1)
                sp.wait_ge(pv_done, NB * PAIRS + 4)
                sp.dma_start(kz[:], scr["ht"][0][0]).then_inc(h0_landed, 16)
                sp.dma_start(qa[:], scr["ht"][1][0, :, 0:HP]).then_inc(h0_landed, 16)
                sp.dma_start(keep["qks"][:], scr["ht"][1][0, :, HP:DC]).then_inc(h0_landed, 16)
            store_x1(b, 0)
            store_x1(b, 1)
            load_residual(b, [4])
            store_x1(b, 2)
            load_residual(b, [5])
            store_x1(b, 3)
            load_residual(b, [6])
            store_ht(b, 0)
            store_x1(b, 4)
            if ahead:
                store_qk(b.next())
            b = b.again(sp, "place")
            load_residual(b, [7])
            if ahead:
                place_qk(b.next())
                b = b.again(sp, "tail")
            store_x1(b, 5)
            store_ht(b, 1)
            store_x1(b, 6)
            store_x1(b, 7)
            store_ht(b, 2)
            store_ht(b, 3)

        each_batch(sp, front, iteration)
        for stored in ht_stored:
            sp.wait_ge(stored, NB * 64 + 1)
        for stored in x1_stored:
            sp.wait_ge(stored, NB * NG * 16 + 1)
        sp.wait_ge(h0_landed, 3 * 16)

    @block.gpsimd
    def _(pool):
        add_credits(pool, credits)
        nc.gpsimd.memset(ident[:], 0.0).then_inc(pool_step, 1)
        pool.wait_ge(pool_step, 1)
        nc.gpsimd.affine_select(out=ident[:], in_=ident[:], compare_op=ALU.not_equal, fill=1.0, base=0,
                                pattern=[[-1, P]], channel_multiplier=1).then_inc(pool_consts, 1)
        nc.gpsimd.memset(half_neg[:], -0.5).then_inc(pool_consts, 1)

        def finish_stats(kind, batch, t):
            pool.wait_ge(stat_ready[kind], batch.n(TT, t + 1))
            nc.gpsimd.tensor_tensor(vare[kind][:, t:t + 1], mv[kind][:, t, 1:2], eps1[:], ALU.add
                                    ).then_inc(vare_ready[kind], 1)
            pool.wait_ge(vare_ready[kind], batch.n(TT, t + 1))
            nc.gpsimd.tensor_tensor(rstd[kind][:, t:t + 1], vare[kind][:, t:t + 1], half_neg[:], ALU.pow
                                    ).then_inc(rstd_ready[kind], 1)
            if kind != "x":
                wait_apart(pool, rstd_ready[kind], batch.n(TT, t + 1), passed)
                nc.gpsimd.tensor_scalar(shift[kind][:, t:t + 1], mv[kind][:, t, 0:1], rstd[kind][:, t:t + 1], -1.0,
                                        ALU.mult, ALU.mult).then_inc(shift_ready[kind], 1)

        def residual(batch, t):
            u = t % GRP
            pool.wait_ge(xres_landed[u], batch.n(NG * 16, (t // GRP + 1) * 16))
            pool.wait_ge(y_norm, batch.n(TT, t + 1))
            nc.gpsimd.tensor_tensor(xres[:, u, :], y4[:, u, :], xres[:, u, :], ALU.add).then_inc(x1_done, 1)

        def front(batch):
            for t in range(TT):
                finish_stats("x", batch, t)

        def tail(batch):
            for s in range(STEPS):
                if 0 <= s - 5 < TT:
                    finish_stats("x1", batch, s - 5)
                if 0 <= s - 3 < TT:
                    residual(batch, s - 3)
                if 0 <= s - 2 < TT:
                    finish_stats("y", batch, s - 2)

        nc.gpsimd.memset(eps1[:], EPS).then_inc(pool_consts, 1)
        pool.wait_ge(pool_consts, 3)
        front(Batch(None, 0))
        nc.gpsimd.memset(ones[:], 1.0).then_inc(pool_consts, 1)
        nc.gpsimd.memset(vision_rows[:], 1.0).then_inc(pool_step, 1)
        pool.wait_ge(pool_step, 2)
        nc.gpsimd.affine_select(out=vision_rows[:], in_=vision_rows[:], compare_op=ALU.is_gt, fill=0.0,
                                base=SPLIT_ROW, pattern=[[0, 1]], channel_multiplier=-1).then_inc(pool_consts, 1)
        nc.gpsimd.memset(mrow[:], 0.0).then_inc(pool_consts, 1)
        nc.gpsimd.memset(qa[:], 0.0).then_inc(pool_consts, 1)
        nc.gpsimd.memset(v32[:, :, :, E:32], 0.0).then_inc(pool_step, 1)
        pool.wait_ge(pool_step, 3)
        nc.gpsimd.memset(v32[:, :, :, E:E + 1], 1.0).then_inc(pool_consts, 1)
        nc.gpsimd.memset(kz[:], 0.0).then_inc(pool_step, 1)
        pool.wait_ge(pool_step, 4)
        for h in range(H):
            v = kz[:, h, :]
            nc.gpsimd.affine_select(out=v, in_=v, compare_op=ALU.not_equal, fill=-1.0,
                                    base=-((h % 2) * HR + 3 * E), pattern=[[0, NT]],
                                    channel_multiplier=1).then_inc(pool_step, 1)
            pool.wait_ge(pool_step, 5 + h)
            nc.gpsimd.affine_select(out=v, in_=v, compare_op=ALU.not_equal, fill=-1.0,
                                    base=-((h % 2) * HR + 3 * E + 1), pattern=[[0, NT]],
                                    channel_multiplier=1).then_inc(pool_consts, 1)
        with pool.Fori(0, NB - 1) as b:
            front(Batch(b).next().again(pool, "front"))
            tail(Batch(b).again(pool, "tail"))
        pool.wait_ge(v_mm, NB * TT)
        for c in range(DC):
            pool.wait_ge(ring_landed[c % STAGE], (c // STAGE + 1) * 16)
            split_weights(nc, pool, xt, c, xa[:, c % STAGE, :], split_step, 2 * c, pool.wait_ge
                          ).then_inc(ring_split, 1)
        tail(Batch(None, NB - 1))

    THREE = ((0, 0), (1, 0), (0, 1))

    @block.tensor
    def _(pe):
        def transpose_tile(slot, banks):
            dst = ps[:, banks:banks + 2, :].rearrange("p a (c q) -> p (a c) q", q=P)
            for c in range(DC):
                last = pe.transpose(dst[:, c, :], xn[:, slot, c * P:(c + 1) * P], ident[:])
            return last

        def front_tile(batch, t):
            pe.wait_ge(front_norm, batch.n(TT, t + 1 + GRP))
            pe.wait_ge(front_lo, batch.n(TT, t + 1))
            transpose_tile(t % 2, FRONT_TP).then_inc(front_tp, 1)

        def qk_unit(batch, n, parts):
            half, m = n // 2, n % 2
            products = [(a, w, c) for a, w in THREE for c in range(DC)]
            for part in parts:
                if part == 0 and n >= 2:
                    pe.wait_ge(qk32_ready, batch.n(4, n - 1))
                for k in range(part * 3 * DC // 2, (part + 1) * 3 * DC // 2):
                    a, w, c = products[k]
                    last = pe.matmul(ps[:, QKV[n % 2], :], wqkv[w][:, c, m * HD:(m + 1) * HD],
                                     xt[a][:, c, half * BANK:(half + 1) * BANK],
                                     start=k == 0, stop=k == 3 * DC - 1)
                if part == 1:
                    last.then_inc(qk_mm, 1)

        def v_unit(batch, u):
            if u < 2:
                pe.wait_ge(qk32_ready, batch.n(4, 3 + u))
            else:
                pe.wait_ge(v_done, batch.n(TT, u - 1))
            k = 0
            for a, w in THREE:
                for c in range(DC):
                    last = pe.matmul(ps[:, QKV[u % 2], 0:HD], xt[a][:, c, u * P:(u + 1) * P],
                                     wqkv[w][:, c, 2 * HD:3 * HD], start=k == 0, stop=k == 3 * DC - 1)
                    k += 1
            last.then_inc(v_mm, 1)

        def front(batch):
            for t in range(TT):
                front_tile(batch, t)
            pe.wait_ge(w_split, 1)
            pe.wait_ge(front_lo, batch.n(TT, TT + 1))
            for n in range(4):
                qk_unit(batch, n, (0, 1))
            for u in range(TT):
                v_unit(batch, u)
            pe.wait_ge(w_split, 3)
            for i in range(WIDE_EARLY):
                wide(batch, i)
            first_maxima(batch, None)

        def wide(b, i):
            if i == 0:
                pe.wait_ge(pool_consts, POOL_CONSTS)
                pe.wait_ge(y_done, b.n(TT, 1))
                pe.wait_ge(v_done, b.n(TT, TT))
                pe.wait_ge(qk_placed, b.n(PLACES * 16, PLACES * 16 + 1))
            qt, h = i // 4, i % 4
            pe.wait_ge(wide_free, b.n(32, i + 1))
            for k in range(HALF):
                last = pe.matmul(ps[:, WIDE[i % 2] + k, :], qa[:, h // 2, qt * P:(qt + 1) * P],
                                 kz[:, h, k * BANK:(k + 1) * BANK], start=True, stop=True)
            last.then_inc(wide_mm, 1)

        def narrow(b, i):
            qt, h, k = i // 8, 4 + i // 2 % 4, i % 2
            pe.wait_ge(narrow_free, b.n(64, i + 1))
            pe.matmul(ps[:, NARROW[i % 2], :], qa[:, h // 2, qt * P:(qt + 1) * P],
                      kz[:, h, k * BANK:(k + 1) * BANK], start=True, stop=True).then_inc(narrow_mm, 1)

        def scores(b, i):
            unit, kt, pair = i // 16, (i // 2) % TT, i % 2
            g, qh = unit // 2, unit % 2
            pe.wait_ge(exp_done, b.n(PAIRS, i + 1))
            for k in range(2):
                h = 4 * g + 2 * pair + k
                last = pe.matmul(ps[:, ST[i % 2] + k, :], kz[:, h, kt * P:(kt + 1) * P],
                                 qa[:, h // 2, qh * BANK:(qh + 1) * BANK], start=True, stop=True)
            last.then_inc(st_ready, 1)

        def values(b, i):
            unit, kt, pair = i // 16, (i // 2) % TT, i % 2
            g = unit // 2
            if i % 16 == 0:
                pe.wait_ge(o_copied, b.n(4, unit + 1))
            pe.wait_ge(exp_done, b.n(PAIRS, i + 3))
            for k in range(2):
                j = 2 * pair + k
                last = pe.matmul(ps[32 * j:32 * (j + 1), O_BANK, :], v32[:, kt, 4 * g + j, :],
                                 p32[:, i % 4, k, :], start=kt == 0, stop=kt == TT - 1)
            last.then_inc(pv_done, 1)

        def back(b, unit):
            pe.wait_ge(o_copied, b.n(4, unit + 2))
            pe.wait_ge(o_norm, b.n(4, unit + 1))
            for q in range(4):
                last = pe.transpose(ps[:, OT_BANK, q * P:(q + 1) * P], osb[:, unit % 2, q * P:(q + 1) * P],
                                    ident[:])
            last.then_inc(ot_done, 1)

        def heads_tile(b, t):
            pe.wait_ge(oolo_done, b.n(TT, t + 1))
            pe.transpose(ps[:, OO_BANK, 0:P], onorm[:, t, :], ident[:]).then_inc(oo_done, 1)

        def output_tile(b, t):
            pe.wait_ge(oolo_done, b.n(TT, t + 2))
            pe.wait_ge(y_done, b.n(TT, t + 1))
            for k in range(2):
                for n, (a, w) in enumerate(THREE):
                    last = pe.matmul(ps[:, Y + k, :], ot[a][:, t % 2, :],
                                     wo[w][:, k * BANK:(k + 1) * BANK], start=n == 0, stop=n == 2)
            last.then_inc(y_mm, 1)

        def tail_tile(b, t):
            pe.wait_ge(tail_norm, b.n(TT, t + 1 + GRP))
            pe.wait_ge(tail_lo, b.n(TT, t + 1))
            transpose_tile(t % 2, TAIL_TP).then_inc(tail_tp, 1)

        def gate_tile(b, t):
            u = t % GRP
            pe.wait_ge(tail_lo, b.n(TT, t + 2))
            k = 0
            for a, w in THREE:
                for c in range(DC):
                    last = pe.matmul(ps[:, GATE_BANK, t * NE:(t + 1) * NE], ht[a][:, c, u * P:(u + 1) * P],
                                     gw[w][:, c, :], start=k == 0, stop=k == 3 * DC - 1)
                    k += 1
            last.then_inc(gate_mm, 1)

        def first_maxima(b, sums_of):
            for i in range(WIDE_EARLY, 32):
                wide(b, i)
                if i == SUMS_AT and sums_of is not None:
                    sums(sums_of)

        def sums(b):
            pe.wait_ge(sums_ready, b.n(1, 1))
            pe.matmul(ps[:, OO_BANK, 0:2], ones[:], parts[:], start=True, stop=True).then_inc(sums_mm, 1)

        def iteration(b, ahead):
            b = b.again(pe, "between")
            pe.wait_ge(tail_lo, b.n(TT, 1))
            pe.wait_ge(o_norm, b.n(4, 1))
            pe.wait_ge(wide_free, b.n(32, 32 + 2))
            pe.transpose(ps[:, OT_BANK, 0:P], mrow[:, 0, :], ident[:]).then_inc(mt_done, 1)
            pe.wait_ge(front_lo, b.n(TT, TT + 1))
            pe.wait_ge(oolo_done, b.n(TT, 1))
            pe.wait_ge(gate_done, b.n(1, 1))
            b = b.again(pe, "first")
            for i in range(NARROW_FIRST):
                narrow(b, i)
            pe.wait_ge(mlo_done, b.n(2, 1))
            pe.wait_ge(m_placed, b.n(128, 64 + 1))
            for i in range(32):
                scores(b, i)
                beside = NARROW_FIRST + 2 * i
                if i <= NARROW_LAST_AT:
                    narrow(b, beside)
                if i >= 2:
                    values(b, i - 2)
                if i <= NARROW_LAST_AT:
                    narrow(b, beside + 1)
                if i in BACK_AT:
                    back(b, BACK_AT[i])
                if i == NARROW_LAST_AT:
                    pe.wait_ge(m_ready, b.n(1, 1))
                    pe.transpose(ps[:, FRONT_TP, 0:P], mrow[:, 1, :], ident[:]).then_inc(mt_done, 1)
            b = b.again(pe, "second")
            pe.wait_ge(mlo_done, b.n(2, 2))
            pe.wait_ge(m_placed, b.n(128, 128 + 1))
            for i in range(32, PAIRS):
                scores(b, i)
                values(b, i - 2)
                if i in BACK_AT:
                    back(b, BACK_AT[i])
                if ahead and i in FRONT_AT:
                    front_tile(b.next(), FRONT_AT[i])
            values(b, PAIRS - 2)
            values(b, PAIRS - 1)
            back(b, 3)
            b = b.again(pe, "tail")
            pe.wait_ge(o_norm, b.n(4, 4 + 1))
            pe.wait_ge(exp_done, b.n(PAIRS, PAIRS + 2))
            if ahead:
                pe.wait_ge(front_lo, b.n(TT, 2 * TT + 1))
            for s in range(STEPS):
                if 0 <= s - 2 < TT:
                    output_tile(b, s - 2)
                if s < TT:
                    heads_tile(b, s)
                if ahead:
                    for n, part in QK_AT.get(s, ()):
                        qk_unit(b.next(), n, (part,))
                    for u in V_AT.get(s, ()):
                        v_unit(b.next(), u)
                if 0 <= s - 5 < TT:
                    tail_tile(b, s - 5)
                if 0 <= s - 7 < TT:
                    gate_tile(b, s - 7)
                if ahead:
                    for i in WIDE_AT.get(s, ()):
                        wide(b.next(), i)
            b = b.again(pe, "maxima")
            if ahead:
                first_maxima(b.next(), b)
            else:
                sums(b)

        pe.wait_ge(pool_consts, 3)
        each_batch(pe, front, iteration)

    @block.scalar
    def _(act):
        def high(dst, t, banks, done):
            src = ps[:, banks:banks + 2, :].rearrange("p a (c q) -> p (a c) q", q=P)
            nc.scalar.activation(dst[:, :, t * P:(t + 1) * P], src, ACT.Copy).then_inc(done, 1)

        def normalise(kind, batch, t, dst, src):
            act.wait_ge(shift_ready[kind], batch.n(TT, t + 1))
            return nc.scalar.activation(dst, src, ACT.Identity, bias=shift[kind][:, t:t + 1],
                                        scale=rstd[kind][:, t:t + 1])

        def front_tile(batch, t):
            act.wait_ge(front_tp, batch.n(TT, t + 3))
            high(xt[0], t, FRONT_TP, front_hi)

        def qk_unit(batch, n):
            act.wait_ge(qk_mm, batch.n(4, n + 1))
            act.wait_ge(qk_split, batch.n(4, n + 1))
            nc.scalar.activation(qk32[:, n % 2, :], ps[:, QKV[n % 2], :], ACT.Identity,
                                 bias=bqk[:, n % 2:n % 2 + 1], scale=1.0 / WS).then_inc(qk32_ready, 1)

        def front(batch):
            for t in range(TT):
                front_tile(batch, t)
            act.wait_ge(const_in, NCONST * 16)
            for n in range(4):
                qk_unit(batch, n)

        def maxima_high(b, g):
            act.wait_ge(mt_done, b.n(2, g + 2))
            act.wait_ge(m_stored, b.n(64, 1))
            bank = (OT_BANK, FRONT_TP)[g]
            nc.scalar.activation(ms[0][:, g, :], ps[:, bank, 0:P], ACT.Copy).then_inc(mhi_done, 1)

        def copy_out(b, unit):
            act.wait_ge(pv_done, b.n(PAIRS, 16 * (unit + 1) + 4))
            act.wait_ge(ot_done, b.n(4, unit + 1))
            nc.scalar.activation(osb[:, unit % 2, :], ps[:, O_BANK, :], ACT.Copy).then_inc(o_copied, 1)

        def probs(b, i):
            act.wait_ge(st_ready, b.n(PAIRS, i + 1))
            act.wait_ge(pv_done, b.n(PAIRS, i + 1))
            nc.scalar.activation(p32[:, i % 4], ps[:, ST[i % 2]:ST[i % 2] + 2, :], ACT.Exp).then_inc(exp_done, 1)
            if i % 16 == 1 and i > 1:
                copy_out(b, i // 16 - 1)

        def iteration(b, ahead):
            b = b.again(act, "first")
            maxima_high(b, 0)
            for i in range(32):
                probs(b, i)
                if i == NARROW_LAST_AT:
                    maxima_high(b, 1)
            b = b.again(act, "second")
            for i in range(32, PAIRS):
                probs(b, i)
            copy_out(b, 3)
            b = b.again(act, "tail")
            act.wait_ge(front_tp, b.n(TT, (2 if ahead else 1) * TT + 2))
            for s in range(STEPS):
                if s < TT:
                    act.wait_ge(oo_done, b.n(TT, s + 1))
                    nc.scalar.activation(ot[0][:, s % 2, :], ps[:, OO_BANK, 0:P], ACT.Copy).then_inc(oohi_done, 1)
                t = s - 3
                if 0 <= t < TT:
                    normalise("y", b, t, y4[:, t % GRP, :], y4[:, t % GRP, :]).then_inc(y_norm, 1)
                t = s - 5
                if 0 <= t < TT:
                    act.wait_ge(tail_tp, b.n(TT, t + 1))
                    act.wait_ge(abs_done, b.n(TT, t + 1))
                    normalise("x1", b, t, xn[:, t % 2, :], xres[:, t % GRP, :]).then_inc(tail_norm, 1)
                for n, part in QK_AT.get(s, ()) if ahead else ():
                    if part == 1:
                        qk_unit(b.next(), n)
                t = s - 5
                if 0 <= t < TT:
                    if t % 2 == 0:
                        act.wait_ge(ht_stored[t // 2 % 2], b.n(64, 32 * (t // GRP) + 1))
                    act.wait_ge(tail_tp, b.n(TT, t + 3))
                    high(ht[0], t % GRP, TAIL_TP, tail_hi)
                    act.wait_ge(abs_done, b.n(TT, t + 2))
                    nc.scalar.activation(habs[:], xn[:, t % 2, :], ACT.Abs, accum_out=asum[:, t:t + 1]
                                         ).then_inc(abs_done, 1)
            act.wait_ge(lg_ready, b.n(1, 1))
            nc.scalar.activation(sc[:], lg[:], ACT.Exp).then_inc(lg_exp, 1)

        each_batch(act, front, iteration)

    @block.vector
    def _(dve):
        steps = {"batch": Batch(None, 0), "before": 0, "now": 0}

        def link(ins):
            steps["now"] += 1
            ins.then_inc(dve_step, 1)
            value = steps["batch"].n(PER_BATCH, steps["before"] + steps["now"])
            if steps["batch"].reg is None:
                dve.wait_ge(dve_step, value)
            else:
                wait_apart(dve, dve_step, value, passed)

        def spaced(ins):
            steps["now"] += 1
            ins.then_inc(dve_step, 1)
            value = steps["batch"].n(PER_BATCH, steps["before"] + steps["now"])
            yield
            if steps["batch"].reg is None:
                dve.wait_ge(dve_step, value)
            else:
                wait_apart(dve, dve_step, value, passed)

        def split(dst_hi, dst_lo, src):
            link(nc.vector.tensor_scalar(dst_hi, src, WS, None, ALU.mult))
            return nc.vector.scalar_tensor_tensor(out=dst_lo, in0=src, scalar=WS, in1=dst_hi, op0=ALU.mult,
                                                  op1=ALU.subtract)

        def tile_stats(kind, t, src):
            for k in range(2):
                last = nc.vector.bn_stats(stats[kind][:, t, k, :], src[:, k * BANK:(k + 1) * BANK])
            link(last)
            nc.vector.bn_aggr(mv[kind][:, t, :], stats[kind][:, t].rearrange("p k s -> p (k s)")
                              ).then_inc(stat_ready[kind], 1)

        def normalise(batch, t, dst, src, kind="x"):
            dve.wait_ge(rstd_ready[kind], batch.n(TT, t + 1))
            return nc.vector.tensor_scalar(dst, src, mv[kind][:, t, 0:1], rstd[kind][:, t:t + 1], ALU.subtract,
                                           ALU.mult)

        def low(dst, t, banks):
            src = ps[:, banks:banks + 2, :].rearrange("p a (c q) -> p (a c) q", q=P)
            return nc.vector.tensor_tensor(dst[1][:, :, t * P:(t + 1) * P], src, dst[0][:, :, t * P:(t + 1) * P],
                                           ALU.subtract)

        def front_stats(batch, t):
            wait_apart(dve, xa_landed[t % GRP], batch.n(NG * 16, (t // GRP + 1) * 16), passed)
            tile_stats("x", t, xa[:, t % GRP, :])

        def front_tile(batch, t, high_too):
            if t < TT:
                dve.wait_ge(front_tp, batch.n(TT, t + 1))
                normalise(batch, t, xn[:, t % 2, :], xa[:, t % GRP, :]).then_inc(front_norm, 1)
            if t + 2 < TT:
                front_stats(batch, t + 2)
            if t:
                if high_too:
                    dve.wait_ge(front_tp, batch.n(TT, t + 2))
                    nc.vector.tensor_copy(xt[0][:, :, (t - 1) * P:t * P], ps[:, FRONT_TP:FRONT_TP + 2, :].rearrange(
                        "p a (c q) -> p (a c) q", q=P)).then_inc(front_hi, 1)
                dve.wait_ge(front_hi, batch.n(TT, t))
                low(xt, t - 1, FRONT_TP).then_inc(front_lo, 1)

        def qk_unit(batch, n):
            half, m = n // 2, n % 2
            cols = slice(half * BANK, (half + 1) * BANK)
            if n == 0:
                dve.wait_ge(qk_stored, batch.n(64, 1))
            dve.wait_ge(qk32_ready, batch.n(4, n + 1))
            link(nc.vector.tensor_copy(qks[m][0][:, cols], qk32[:, n % 2, :]))
            nc.vector.tensor_tensor(qks[m][1][:, cols], qk32[:, n % 2, :], qks[m][0][:, cols],
                                    ALU.subtract).then_inc(qk_split, 1)

        def v_unit(batch, t):
            dve.wait_ge(v_mm, batch.n(TT, t + 1))
            nc.vector.scalar_tensor_tensor(
                out=v32[:, t, :, 0:E], in0=ps[:, QKV[t % 2], 0:HD].rearrange("p (h e) -> p h e", h=H),
                scalar=1.0 / WS, in1=bv[:].rearrange("p (h e) -> p h e", h=H), op0=ALU.mult,
                op1=ALU.add).then_inc(v_done, 1)

        def front(batch):
            front_stats(batch, 0)
            front_stats(batch, 1)
            for t in range(TT + 1):
                front_tile(batch, t, False)
                if t == TT // 2:
                    dve.wait_ge(wqkv_in, 16)
                    split(wqkv[0][:], wqkv[1][:], wqkv32).then_inc(w_split, 1)
            dve.wait_ge(const_in, NCONST * 16)
            split(wo[0][:], wo[1][:], wo32).then_inc(w_split, 1)
            split(gw[0][:], gw[1][:], gstage[:]).then_inc(w_split, 1)
            for n in range(4):
                qk_unit(batch, n)
            for t in range(TT):
                v_unit(batch, t)
            steps["before"], steps["now"] = steps["now"], 0
            dve.wait_ge(pool_consts, POOL_CONSTS)
            for i in range(WIDE_EARLY):
                wide(batch, i)
            first_maxima(batch, iter(()))

        def wide(b, i):
            qt, h = i // 4, i % 4
            if i == 0:
                dve.wait_ge(mt_done, b.n(2, 1))
            dve.wait_ge(wide_mm, b.n(32, i + 1))
            nc.vector.reduce_max(mrow[:, 0, h * TT + qt:h * TT + qt + 1],
                                 ps[:, WIDE[i % 2]:WIDE[i % 2] + 2, :].rearrange("p a n -> p (a n)"),
                                 AX.X).then_inc(wide_free, 1)

        def first_maxima(b, gate_steps):
            for i in range(WIDE_EARLY, 32):
                wide(b, i)
                next(gate_steps, None)
            for _ in gate_steps:
                pass

        def maxima_low(b, g):
            dve.wait_ge(mhi_done, b.n(2, g + 1))
            bank = (OT_BANK, FRONT_TP)[g]
            nc.vector.tensor_tensor(ms[1][:, g, :], ps[:, bank, 0:P], ms[0][:, g, :], ALU.subtract
                                    ).then_inc(mlo_done, 1)

        def narrow(b, i):
            dve.wait_ge(narrow_mm, b.n(64, i + 1))
            qt, h, k = i // 8, i // 2 % 4, i % 2
            return nc.vector.reduce_max(mpart[:, h * TT + qt, k:k + 1], ps[:, NARROW[i % 2], :], AX.X
                                        ).then_inc(narrow_free, 1)

        def head_outputs(b, unit):
            g, qh = unit // 2, unit % 2
            dve.wait_ge(ot_done, b.n(4, unit + 3))
            o4 = ps[:, OT_BANK, :].rearrange("p (q j e) -> p q j e", q=4, j=4)
            link(nc.vector.reciprocal(rinv[:], o4[:, :, :, E:E + 1]))
            for q in range(4):
                last = nc.vector.tensor_tensor(
                    onorm[:, 4 * qh + q, 4 * E * g:4 * E * (g + 1)].rearrange("p (j e) -> p j e", j=4),
                    o4[:, q, :, 0:E], rinv[:, q].to_broadcast([P, 4, E]), ALU.mult)
            last.then_inc(o_norm, 1)

        def tail_step(b, s, ahead):
            t = s - 1
            if 0 <= t < TT:
                dve.wait_ge(oohi_done, b.n(TT, t + 1))
                nc.vector.tensor_tensor(ot[1][:, t % 2, :], ps[:, OO_BANK, 0:P], ot[0][:, t % 2, :],
                                        ALU.subtract).then_inc(oolo_done, 1)
            t = s - 6
            if 0 <= t < TT:
                dve.wait_ge(tail_hi, b.n(TT, t + 1))
                low(ht, t % GRP, TAIL_TP).then_inc(tail_lo, 1)
            t = s - 2
            if 0 <= t < TT:
                dve.wait_ge(x1_done, b.n(TT, t + 1))
                dve.wait_ge(y_mm, b.n(TT, t + 1))
                nc.vector.scalar_tensor_tensor(
                    out=y4[:, t % GRP, :], in0=ps[:, Y:Y + 2, :].rearrange("p a n -> p (a n)"),
                    scalar=1.0 / (WS * float(HD) ** 0.5), in1=bo[:], op0=ALU.mult, op1=ALU.add).then_inc(y_done, 1)
                wait_apart(dve, y_done, b.n(TT, t + 2), passed)
                tile_stats("y", t, y4[:, t % GRP, :])
            t = s - 4
            if 0 <= t < TT:
                wait_apart(dve, x1_done, b.n(TT, t + 1 + GRP), passed)
                tile_stats("x1", t, xres[:, t % GRP, :])
            if ahead:
                for n, part in QK_AT.get(s - 1, ()):
                    if part == 1:
                        qk_unit(b.next(), n)
                for u in V_AT.get(s, ()):
                    v_unit(b.next(), u)
                for i in WIDE_AT.get(s, ()):
                    wide(b.next(), i)

        def gate(b):
            yield
            dve.wait_ge(abs_done, b.n(TT, TT + 2))
            nc.vector.reduce_sum(gs[:, 0:1], asum[:, 0:SPLIT_TILE], AX.X)
            yield from spaced(nc.vector.reduce_sum(gs[:, 1:2], asum[:, SPLIT_TILE:TT], AX.X))
            yield from spaced(nc.vector.tensor_tensor(gs[:, 2:3], asum[:, SPLIT_TILE:SPLIT_TILE + 1], vision_rows[:], ALU.mult))
            nc.vector.tensor_tensor(parts[:, 0:1], gs[:, 0:1], gs[:, 2:3], ALU.add)
            nc.vector.tensor_tensor(parts[:, 1:2], gs[:, 1:2], gs[:, 2:3], ALU.subtract).then_inc(sums_ready, 1)
            yield
            dve.wait_ge(sums_mm, b.n(1, 1))
            yield from spaced(nc.vector.tensor_scalar(gs[:, 3:4], ps[:, OO_BANK, 0:1], 1.0 / (VISION * D), 1e-8, ALU.mult, ALU.add))
            yield from spaced(nc.vector.reciprocal(gs[:, 4:5], gs[:, 3:4]))
            yield from spaced(nc.vector.scalar_tensor_tensor(out=gs[:, 5:6], in0=ps[:, OO_BANK, 1:2], scalar=1.0 / ((NT - VISION) * D),
                                                in1=gs[:, 4:5], op0=ALU.mult, op1=ALU.mult))
            yield from spaced(nc.vector.scalar_tensor_tensor(out=gbase[:], in0=gw_ratio[:], scalar=gs[:, 5:6], in1=gate_b[:],
                                                op0=ALU.mult, op1=ALU.add))
            dve.wait_ge(gate_mm, b.n(TT, TT))
            yield from spaced(nc.vector.scalar_tensor_tensor(
                out=lg[:], in0=ps[:, GATE_BANK, 0:TT * NE].rearrange("p (t e) -> p t e", e=NE), scalar=1.0 / WS,
                in1=gbase[:].unsqueeze(1).to_broadcast([P, TT, NE]), op0=ALU.mult, op1=ALU.add))
            g2 = g1[:].unsqueeze(3)
            yield from spaced(nc.vector.reduce_max(g2[:, 0], lg[:], AX.X))
            nc.vector.tensor_tensor(lg[:], lg[:], g2[:, 0].to_broadcast([P, TT, NE]), ALU.subtract
                                    ).then_inc(lg_ready, 1)
            yield
            dve.wait_ge(lg_exp, b.n(1, 1))
            yield from spaced(nc.vector.reduce_sum(g2[:, 1], sc[:], AX.X))
            yield from spaced(nc.vector.reciprocal(g2[:, 2], g2[:, 1]))
            yield from spaced(nc.vector.tensor_tensor(sc[:], sc[:], g2[:, 2].to_broadcast([P, TT, NE]), ALU.mult))
            nc.vector.reduce_max(g2[:, 3], sc[:], AX.X)
            nc.vector.tensor_tensor(g2[:, 4], sc[:, :, 0:1], sc[:, :, 1:2], ALU.min)
            yield from spaced(nc.vector.tensor_tensor(g2[:, 5], sc[:, :, 0:1], sc[:, :, 1:2], ALU.max))
            yield from spaced(nc.vector.tensor_tensor(g2[:, 5], g2[:, 5], sc[:, :, 2:3], ALU.min))
            yield from spaced(nc.vector.tensor_tensor(g2[:, 4], g2[:, 4], g2[:, 5], ALU.max))
            yield from spaced(nc.vector.scalar_tensor_tensor(out=g2[:, 6], in0=g2[:, 3], scalar=1e-8, in1=g2[:, 4],
                                                op0=ALU.add, op1=ALU.add))
            yield from spaced(nc.vector.reciprocal(g2[:, 7], g2[:, 6]))
            for k in range(2):
                nc.vector.tensor_tensor(keep["tv"][:, bass.ds(b.n(2 * TT, k * TT), TT)], g1[:, 3 + k, :],
                                        g1[:, 7, :], ALU.mult)
            a, c, d = (sc[0:1, 0, k:k + 1] for k in range(NE))

            def flag(k, x, y, op):
                return nc.vector.tensor_tensor(jt[:, k:k + 1], x, y, op)

            flag(0, a, c, ALU.is_ge)
            flag(1, a, d, ALU.is_ge)
            flag(2, c, d, ALU.is_ge)
            flag(3, c, a, ALU.is_le)
            flag(4, d, a, ALU.is_le)
            yield from spaced(flag(5, d, c, ALU.is_le))
            flag(6, jt[:, 0:1], jt[:, 1:2], ALU.mult)
            yield from spaced(flag(7, jt[:, 4:5], jt[:, 5:6], ALU.mult))
            nc.vector.tensor_scalar(jt[:, 8:9], jt[:, 6:7], -1.0, 1.0, ALU.mult, ALU.add)
            nc.vector.tensor_scalar(jt[:, 9:10], jt[:, 2:3], -1.0, 2.0, ALU.mult, ALU.add)
            yield from spaced(nc.vector.tensor_scalar(jt[:, 10:11], jt[:, 3:4], -1.0, 2.0, ALU.mult, ALU.add))
            flag(11, jt[:, 8:9], jt[:, 9:10], ALU.mult)
            yield from spaced(flag(12, jt[:, 7:8], jt[:, 10:11], ALU.mult))
            yield from spaced(flag(13, jt[:, 12:13], jt[:, 3:4], ALU.add))
            yield from spaced(flag(14, jt[:, 11:12], jt[:, 13:14], ALU.add))
            nc.vector.tensor_copy(keep["jobs"][:, bass.ds(b.n(2), 1)], jt[:, 11:12])
            nc.vector.tensor_scalar(keep["jobs"][:, bass.ds(b.n(2, 1), 1)], jt[:, 14:15], -1.0, 3.0, ALU.mult,
                                    ALU.add).then_inc(gate_done, 1)

        def iteration(b, ahead):
            steps["batch"], steps["now"] = b, 0
            maxima_low(b, 0)
            b = b.again(dve, "first")
            steps["batch"] = b
            backs = {NARROW_FIRST + 2 * (i + 2): unit for i, unit in BACK_AT.items()}
            for i in range(64):
                if i in backs:
                    head_outputs(b, backs[i])
                narrow(b, i)
            dve.wait_ge(narrow_free, b.n(64, 64 + 2))
            nc.vector.tensor_tensor(mrow[:, 1, 0:32], mpart[:, :, 0], mpart[:, :, 1], ALU.max).then_inc(m_ready, 1)
            maxima_low(b, 1)
            b = b.again(dve, "second")
            steps["batch"] = b
            if ahead:
                front_stats(b.next(), 0)
                front_stats(b.next(), 1)
                dve.wait_ge(tail_tp, b.n(TT, 2))
                dve.wait_ge(abs_done, b.n(TT, 2))
                for t in range(TT + 1):
                    front_tile(b.next(), t, True)
                    if t == 1:
                        head_outputs(b, 1)
                    if t == 5:
                        head_outputs(b, 2)
            else:
                head_outputs(b, 1)
                head_outputs(b, 2)
            head_outputs(b, 3)
            b = b.again(dve, "tail")
            steps["batch"] = b
            for s in range(STEPS):
                tail_step(b, s, ahead)
                if s == STEPS // 2:
                    b = b.again(dve, "tail_end")
                    steps["batch"] = b
            b = b.again(dve, "gate")
            steps["batch"] = b
            if ahead:
                first_maxima(b.next(), gate(b))
            for _ in gate(b) if not ahead else ():
                pass
            if ahead:
                assert steps["now"] == PER_BATCH, steps["now"]

        each_batch(dve, front, iteration)


PER_BATCH = 54


def expert_phase(nc, io, scr, keep, out, ctx):

    def sb(name, shape, dt=F32):
        return ctx.enter_context(nc.sbuf_tensor(name, shape, dt))

    def sem(name):
        return ctx.enter_context(nc.semaphore(name))

    ps1 = ctx.enter_context(nc.psum_tensor("ps1", [P, 2, NT], F32))
    ps2 = ctx.enter_context(nc.psum_tensor("ps2", [P, 2, D], F32))
    JOBS = 2 * NB

    stage = keep["ring"]
    w1 = keep["wide16"]
    w2 = [sb(f"w2{i}", [P, DC, D], F16) for i in range(2)]
    ht = [[keep["kz"][:, c] for c in range(DC)],
          [keep["qa"][:, c] for c in range(HP)] + [keep["qks"][:, c] for c in range(DC - HP)]]
    ht_places = ((keep["kz"], 0, 0, DC), (keep["qa"], 1, 0, HP), (keep["qks"], 1, HP, DC))
    hid = [sb(f"hid{i}", [P, DC, NT], F16) for i in range(2)]
    act32 = sb("act32", [P, 2, NT])
    b2bc = sb("b2bc", [P, D])
    etmp = sb("etmp", [P, 2, D])
    moe = sb("moe", [P, TT, D])
    x1b = sb("x1b", [P, D])
    stats = sb("stats2", [P, 2, 2, 6])
    mv = sb("mv2", [P, 2, 2])
    std = sb("std2", [P, 2])
    rstd = sb("rstd2", [P, 2])
    epsc = sb("epsc", [P, 1])

    stage_landed = [sem(f"stage_landed{i}") for i in range(STAGE)]
    chunk_split = sem("chunk_split")
    pool_step2 = sem("pool_step2")
    ht_landed = sem("ht_landed")
    b2_landed = sem("b2_landed")
    mm1_done = sem("mm1_done")
    mm2_done = sem("mm2_done")
    act_done = sem("act_done")
    hidden_hi = sem("hidden_hi")
    hidden_split = sem("hidden_split")
    evac_done = sem("evac_done")
    etmp_done = sem("etmp_done")
    eps_ready = sem("eps_ready")
    var_ready = sem("var_ready")
    std_ready = sem("std_ready")
    dve_step2 = sem("dve_step2")
    x1_landed = sem("x1_landed")
    norm_done = sem("norm_done")
    y_ready = sem("y_ready")
    y_stored = [sem(f"y_stored{i}") for i in range(2)]
    passed2 = sem("passed2")

    w_dram = (io["w1"].rearrange("e (c p) n -> e c p n", p=P), io["w2"].rearrange("e (c p) n -> e c p n", p=P))
    out_v = out.rearrange("b (t p) d -> (b t) p d", p=P)
    x1_v = scr["x1"].rearrange("b (t p) d -> (b t) p d", p=P)
    block = ctx.enter_context(nc.Block())

    @block.sync
    def _(sp):
        def load_weights(b, s, which, before):
            e = sp.value_load(keep["jobs"][:, bass.ds(b.n(2, s), 1)], min_val=0, max_val=NE - 1)
            for c in range(DC):
                sp.wait_ge(chunk_split, b.n(4 * DC, before + c + 1))
                sp.dma_start(stage[:, c % STAGE, :], w_dram[which][bass.ds(e, 1), c].rearrange("o p n -> (o p) n")
                             ).then_inc(stage_landed[c % STAGE], 16)
                if which == 1 and c == STAGE - 1:
                    sp.wait_ge(evac_done, b.n(2 * TT, s * TT + 2))
                    sp.dma_start(b2bc[:], io["b2"][bass.ds(e, 1)].to_broadcast([P, D])).then_inc(b2_landed, 16)

        def load_h(b):
            for place, part, first, end in ht_places:
                sp.dma_start(place[:], scr["ht"][part][bass.ds(b.n(1), 1), :, first:end]
                             .rearrange("o p c t -> (o p) c t")).then_inc(ht_landed, 16)

        def iteration(b, ahead):
            load_weights(b, 0, 1, 0)
            load_weights(b, 1, 0, DC)
            load_weights(b, 1, 1, 2 * DC)
            if ahead:
                b = b.again(sp, "next")
                sp.wait_ge(mm1_done, b.n(2 * TT, 2 * TT + 1))
                load_h(b.next())
                load_weights(b, 2, 0, 3 * DC)

        with sp.Fori(0, NB - 1) as b:
            iteration(Batch(b), True)
        iteration(Batch(None, NB - 1), False)

    @block.gpsimd
    def _(pool):
        add_credits(pool, [(chunk_split, STAGE), (act_done, 2), (hidden_split, 2), (evac_done, 2),
                           (mm1_done, 1), (mm2_done, 1), (y_ready, 1), (y_stored[0], 1), (y_stored[1], 1),
                           (ht_landed, 3 * 16)])

        def layer(job, which):
            pool.wait_ge((mm1_done, mm2_done)[which], job.n(TT, (1 - which) * TT + 1))
            for c in range(DC):
                k = (1 - which) * DC + c
                wait_apart(pool, stage_landed[c % STAGE], job.n(2 * DC // STAGE * 16, (k // STAGE + 1) * 16), passed2)
                split_weights(nc, pool, (w1, w2)[which], c, stage[:, c % STAGE, :], pool_step2,
                              job.n(4 * DC, 2 * k), lambda s, v: wait_apart(pool, s, v, passed2)
                              ).then_inc(chunk_split, 1)

        with pool.Fori(0, JOBS - 1) as job:
            layer(Batch(job), 1)
            layer(Batch(job), 0)
        layer(Batch(None, JOBS - 1), 1)

    @block.tensor
    def _(pe):
        with pe.Fori(0, NB) as b:
            for s in range(2):
                if s == 0:
                    pe.wait_ge(ht_landed, (b + 1) * (3 * 16))
                wait_apart(pe, chunk_split, b * (4 * DC) + (s * 2 * DC + STAGE), passed2)
                with pe.Fori(0, TT // 2) as pair:
                    f0 = pair * 2
                    for u in range(2):
                        pe.wait_ge(act_done, b * (2 * TT) + f0 + (s * TT + u + 1))
                        for half in range(HALF):
                            k = 0
                            for a, w in ((0, 0), (1, 0), (0, 1)):
                                for c in range(DC):
                                    last = pe.matmul(ps1[:, u, half * BANK:(half + 1) * BANK],
                                                     w1[w][:, c, bass.ds(f0 * P + u * P, P)],
                                                     ht[a][c][:, half * BANK:(half + 1) * BANK],
                                                     start=k == 0, stop=k == 3 * DC - 1)
                                    k += 1
                        last.then_inc(mm1_done, 1)
                pe.wait_ge(chunk_split, b * (4 * DC) + (s * 2 * DC + DC + STAGE))
                wait_apart(pe, hidden_split, b * (2 * TT) + ((s + 1) * TT + 1), passed2)
                with pe.Fori(0, TT // 2) as pair:
                    t0 = pair * 2
                    for u in range(2):
                        pe.wait_ge(evac_done, b * (2 * TT) + t0 + (s * TT + u + 1))
                        for half in range(HALF):
                            k = 0
                            for c in range(DC):
                                if c == DC - 1 and half == 0 and u == 0:
                                    pe.wait_ge(hidden_split, b * (2 * TT) + ((s + 1) * TT + 2))
                                for a, w in ((0, 0), (1, 0), (0, 1)):
                                    last = pe.matmul(ps2[:, u, half * BANK:(half + 1) * BANK],
                                                     hid[a][:, c, bass.ds(t0 * P + u * P, P)],
                                                     w2[w][:, c, half * BANK:(half + 1) * BANK],
                                                     start=k == 0, stop=k == 3 * DC - 1)
                                    k += 1
                        last.then_inc(mm2_done, 1)

    @block.scalar
    def _(act):
        def hidden_tiles(b, s, e, func):
            with act.Fori(0, TT // 2) as pair:
                f0 = pair * 2
                for u in range(2):
                    act.wait_ge(mm1_done, b * (2 * TT) + f0 + (s * TT + u + 1) + 1)
                    act.wait_ge(hidden_split, b * (2 * TT) + f0 + (s * TT + u + 1))
                    nc.scalar.activation(act32[:, u, :], ps1[:, u, :], func,
                                         bias=keep["b1"][:, bass.ds(f0 + (e * DC + u), 1)], scale=1.0 / WS
                                         ).then_inc(act_done, 1)

        act.wait_ge(eps_ready, 1)
        with act.Fori(0, NB) as b:
            for s in range(2):
                j = act.value_load(keep["jobs"][:, bass.ds(b * 2 + s, 1)], min_val=0, max_val=NE - 1)
                for e, func in enumerate((ACT.Tanh, ACT.Gelu, ACT.Silu)):
                    with act.If(j == e):
                        hidden_tiles(b, s, e, func)
            with act.Fori(0, TT // 2) as pair:
                for u in range(2):
                    t = b * TT + pair * 2 + u
                    act.wait_ge(y_ready, t + 1)
                    act.dma_start(x1b[:], x1_v[bass.ds(t, 1)].rearrange("o p d -> (o p) d")).then_inc(x1_landed, 16)
                    act.wait_ge(var_ready, t + 1)
                    nc.scalar.activation(std[:, u:u + 1], mv[:, u, 1:2], ACT.Sqrt, bias=epsc[:]
                                         ).then_inc(std_ready, 1)
                    act.wait_ge(y_ready, t + 2)
                    act.dma_start(out_v[bass.ds(t, 1)].rearrange("o p d -> (o p) d"), etmp[:, u, :]
                                  ).then_inc(y_stored[u], 16)
        for u in range(2):
            act.wait_ge(y_stored[u], NB * TT // 2 * 16 + 1)

    @block.vector
    def _(dve):
        nc.vector.memset(epsc[:], EPS).then_inc(eps_ready, 1)
        with dve.Fori(0, NB) as b:
            for s in range(2):
                wait_apart(dve, mm2_done, b * (2 * TT) + s * TT + 1, passed2)
                with dve.Fori(0, TT // 2) as pair:
                    f0 = pair * 2
                    for u in range(2):
                        n = b * (2 * TT) + f0 + (s * TT + u)
                        dve.wait_ge(act_done, n + 3)
                        nc.vector.tensor_copy(hid[0][:, bass.ds(f0 + u, 1), :].rearrange("p o n -> p (o n)"),
                                              act32[:, u, :]).then_inc(hidden_hi, 1)
                        dve.wait_ge(hidden_hi, n + 1)
                        nc.vector.tensor_tensor(hid[1][:, bass.ds(f0 + u, 1), :].rearrange("p o n -> p (o n)"),
                                                act32[:, u, :],
                                                hid[0][:, bass.ds(f0 + u, 1), :].rearrange("p o n -> p (o n)"),
                                                ALU.subtract).then_inc(hidden_split, 1)
                wait_apart(dve, b2_landed, b * 32 + (s + 1) * 16, passed2)
                if s == 0:
                    for u in range(2):
                        wait_apart(dve, y_stored[u], b * (TT // 2 * 16) + 1, passed2)
                with dve.Fori(0, TT // 2) as pair:
                    t0 = pair * 2
                    for u in range(2):
                        n = b * (2 * TT) + t0 + (s * TT + u)
                        m = moe[:, bass.ds(t0 + u, 1), :].rearrange("p o n -> p (o n)")
                        tv = keep["tv"][:, bass.ds(b * (2 * TT) + t0 + (s * TT + u), 1)]
                        if s == 1:
                            wait_apart(dve, y_stored[u], b * (TT // 2 * 16) + pair * 16 + 1, passed2)
                        dve.wait_ge(mm2_done, n + 2)
                        nc.vector.scalar_tensor_tensor(out=etmp[:, u, :], in0=ps2[:, u, :], scalar=1.0 / WS,
                                                       in1=b2bc[:], op0=ALU.mult, op1=ALU.add
                                                       ).then_inc(evac_done, 1)
                        dve.wait_ge(evac_done, n + 3)
                        if s == 0:
                            nc.vector.tensor_scalar(m, etmp[:, u, :], tv, None, ALU.mult).then_inc(etmp_done, 1)
                            continue
                        nc.vector.scalar_tensor_tensor(out=etmp[:, u, :], in0=etmp[:, u, :], scalar=tv, in1=m,
                                                       op0=ALU.mult, op1=ALU.add).then_inc(etmp_done, 1)
                        t = b * TT + t0 + u
                        wait_apart(dve, etmp_done, n + 1, passed2)
                        for k in range(2):
                            last = nc.vector.bn_stats(stats[:, u, k, :], etmp[:, u, k * BANK:(k + 1) * BANK])
                        last.then_inc(dve_step2, 1)
                        wait_apart(dve, dve_step2, t * 2 + 1, passed2)
                        nc.vector.bn_aggr(mv[:, u, :], stats[:, u].rearrange("p k s -> p (k s)")).then_inc(var_ready, 1)
                        dve.wait_ge(std_ready, t + 1)
                        nc.vector.reciprocal(rstd[:, u:u + 1], std[:, u:u + 1]).then_inc(dve_step2, 1)
                        dve.wait_ge(dve_step2, t * 2 + 2)
                        nc.vector.tensor_scalar(etmp[:, u, :], etmp[:, u, :], mv[:, u, 0:1], rstd[:, u:u + 1],
                                                ALU.subtract, ALU.mult).then_inc(norm_done, 1)
                        wait_apart(dve, norm_done, t + 1, passed2)
                        dve.wait_ge(x1_landed, (t + 1) * 16)
                        nc.vector.tensor_tensor(etmp[:, u, :], etmp[:, u, :], x1b[:], ALU.add).then_inc(y_ready, 1)


def sandwich_block(nc, io, out):
    with ExitStack() as ctx:
        keep = {
            "tv": ctx.enter_context(nc.sbuf_tensor("tv", [P, NB * 2 * TT], F32)),
            "jobs": ctx.enter_context(nc.sbuf_tensor("jobs", [1, NB * 2], I32)),
            "b1": ctx.enter_context(nc.sbuf_tensor("b1", [P, NE * DC], F32)),
            "ring": ctx.enter_context(nc.sbuf_tensor("ring", [P, STAGE, D], F32)),
            "wide16": [ctx.enter_context(nc.sbuf_tensor(f"wide16_{i}", [P, DC, NT], F16)) for i in range(2)],
            "kz": ctx.enter_context(nc.sbuf_tensor("kz", [P, H, NT], F16)),
            "qa": ctx.enter_context(nc.sbuf_tensor("qa", [P, HP, NT], F16)),
            "qks": ctx.enter_context(nc.sbuf_tensor("qks", [P, 4, NT], F16)),
        }
        scr = {
            "qk": nc.dram_tensor("scr_qk", (2, 2, HD, NT), F16).ap(),
            "m": nc.dram_tensor("scr_m", (2, 2, H * TT // 2, P), F16).ap(),
            "x1": nc.dram_tensor("scr_x1", (NB, NT, D), F32).ap(),
            "ht": [nc.dram_tensor(f"scr_ht{i}", (NB, P, DC, NT), F16).ap() for i in range(2)],
        }
        with ExitStack() as phase:
            attention_phase(nc, io, scr, keep, phase)
        with ExitStack() as phase:
            expert_phase(nc, io, scr, keep, out, phase)


def kernel(**inputs):
    import numpy as np
    import concourse.bacc as bacc
    from concourse import mybir as mb
    from concourse.bass_utils import run_bass_kernel_spmd

    a = {k[3:]: np.asarray(v) for k, v in inputs.items()}
    wqk = a["attn_Wqk_w"].reshape(HD, 2, D).transpose(1, 0, 2).reshape(2 * HD, D)
    arrays = {
        "x": a["attn_x"],
        "wqkv_t": np.concatenate([wqk, a["attn_Wv_w"]], 0).T,
        "bqk": a["attn_Wqk_b"].reshape(HD, 2),
        "bv": a["attn_Wv_b"],
        "wo_t": a["attn_Wo_w"].T,
        "bo": a["attn_Wo_b"],
        "gate_w": a["ffn_gate_w"][:D],
        "gw_ratio": a["ffn_gate_w"][D],
        "gate_b": a["ffn_gate_b"],
        "w1": a["ffn_w1"],
        "b1": a["ffn_b1"].reshape(NE, DC, P).transpose(2, 0, 1).reshape(P, NE * DC),
        "w2": a["ffn_w2"],
        "b2": a["ffn_b2"],
    }
    arrays = {k: np.ascontiguousarray(v) for k, v in arrays.items()}
    nc = bacc.Bacc("TRN2", target_bir_lowering=False, num_devices=1)
    io = {k: nc.dram_tensor(f"in_{k}", v.shape, mb.dt.from_np(v.dtype), kind="ExternalInput").ap()
          for k, v in arrays.items()}
    out = nc.dram_tensor("out", (NB, NT, D), mb.dt.float32, kind="ExternalOutput").ap()
    sandwich_block(nc, io, out)
    r = run_bass_kernel_spmd(nc, [{f"in_{k}": v for k, v in arrays.items()}], core_ids=[0])
    return r.results[0]["out"]
```
